# Optimizing a Trainium2 kernel written in Bass

```python
import numpy as np
import jax
import jax.numpy as jnp

def _softmax(x, axis=-1):
    return jax.nn.softmax(x, axis=axis)

def _gelu(x):
    return jax.nn.gelu(x, approximate=True)

def _silu(x):
    return jax.nn.silu(x)

def _sigmoid(x):
    return jax.nn.sigmoid(x)

def _layernorm(x, axis=-1, eps=1e-05):
    m = jnp.mean(x, axis=axis, keepdims=True)
    v = jnp.var(x, axis=axis, keepdims=True)
    return (x - m) / jnp.sqrt(v + eps)

def _scatter_add(tgt, idx, src, axis=0):
    return tgt.at[idx].add(src)

def _segment_sum(src, seg, n):
    return jax.ops.segment_sum(src, seg, n)
kernel_name = 'mk_gnn_ffn_d1_gnn_r8_aaa181'

def setup_inputs(seed: int=0):
    np.random.seed(seed)
    _w = jnp.asarray

    def _rec_inputs():
        import jax
        import jax.numpy as jnp
        _gk = jax.random.key(seed)
        x = -6.415e-05 + 1 * jax.random.normal(jax.random.fold_in(_gk, 1), (1250, 512), jnp.float32)
        src = jax.random.randint(jax.random.fold_in(_gk, 2), (20000,), 0, 1250, jnp.int32)
        dst = jnp.minimum((1250 * jax.random.uniform(jax.random.fold_in(_gk, 3), (20000,)) ** 2.0).astype(jnp.int32), 9999)
        _o = jnp.argsort(dst, stable=True)
        src = src[_o]
        dst = dst[_o]
        return (x, src, dst)
    x, src, dst = _rec_inputs()

    def _L0_gnn_setup():
        import jax, jax.numpy as jnp
        import numpy as np
        N, E, D_IN, D_H = (2500, 40000, 512, 512)
        ALPHA = 0.1
        LAMBDA = 1.0

        def _gcn2_layer(h, h0, src, dst, norm, w1, w2, b, layer):
            beta = float(np.log(LAMBDA / layer + 1.0))
            x = h * norm
            agg = jax.ops.segment_sum(x[src], dst, num_segments=h.shape[0])
            agg = agg * norm
            f = agg * (1.0 - ALPHA)
            f0 = h0 * ALPHA
            rst = (1.0 - beta) * f + beta * (f @ w1) + (1.0 - beta) * f0 + beta * (f0 @ w2) + b
            return jax.nn.relu(rst)
        key = jax.random.key(seed)
        ks = jax.random.split(key, 12)
        feat = jax.random.normal(ks[0], (N, D_IN), dtype=jnp.float32)
        src = jax.random.randint(ks[1], (E,), 0, N, dtype=jnp.int32)
        dst = jax.random.randint(ks[2], (E,), 0, N, dtype=jnp.int32)
        s = 0.05
        fc_w = jax.random.normal(ks[3], (D_H, D_IN), dtype=jnp.float32) * s
        fc_b = jax.random.normal(ks[4], (D_H,), dtype=jnp.float32) * s
        w1_1 = jax.random.normal(ks[5], (D_H, D_H), dtype=jnp.float32) * s
        w2_1 = jax.random.normal(ks[6], (D_H, D_H), dtype=jnp.float32) * s
        b_1 = jax.random.normal(ks[7], (D_H,), dtype=jnp.float32) * s
        w1_2 = jax.random.normal(ks[8], (D_H, D_H), dtype=jnp.float32) * s
        w2_2 = jax.random.normal(ks[9], (D_H, D_H), dtype=jnp.float32) * s
        b_2 = jax.random.normal(ks[10], (D_H,), dtype=jnp.float32) * s
        return {'feat': feat, 'src': src, 'dst': dst, 'fc_w': fc_w, 'fc_b': fc_b, 'w1_1': w1_1, 'w2_1': w2_1, 'b_1': b_1, 'w1_2': w1_2, 'w2_2': w2_2, 'b_2': b_2}
    _L0_gnn_all = _L0_gnn_setup()
    _L0_gnn_in = {k: v for k, v in _L0_gnn_all.items() if k in ('fc_w', 'fc_b', 'w1_1', 'w2_1', 'b_1', 'w1_2', 'w2_2', 'b_2')}
    del _L0_gnn_all

    def _L0_ffn_setup():
        import jax, jax.numpy as jnp
        import numpy as np
        INPUT_SIZE = 512
        HIDDEN_SIZE = 512
        key = jax.random.key(seed)
        ks = jax.random.split(key, 9)
        B, T, I, H = (64, 512, INPUT_SIZE, HIDDEN_SIZE)
        scale = 1.0 / np.sqrt(I + H)
        x = jax.random.normal(ks[0], (B, T, I), dtype=jnp.float32)

        def lin(kw, kb):
            W = jax.random.uniform(kw, (I + H, H), minval=-scale, maxval=scale, dtype=jnp.float32)
            b = jax.random.uniform(kb, (H,), minval=-scale, maxval=scale, dtype=jnp.float32)
            return (W, b)
        W_f, b_f = lin(ks[1], ks[2])
        W_i, b_i = lin(ks[3], ks[4])
        W_c, b_c = lin(ks[5], ks[6])
        W_o, b_o = lin(ks[7], ks[8])
        return {'x': x, 'W_f': W_f, 'b_f': b_f, 'W_i': W_i, 'b_i': b_i, 'W_c': W_c, 'b_c': b_c, 'W_o': W_o, 'b_o': b_o}
    _L0_ffn_all = _L0_ffn_setup()
    _L0_ffn_in = {k: v for k, v in _L0_ffn_all.items() if k in ('W_f', 'b_f', 'W_i', 'b_i', 'W_c', 'b_c', 'W_o', 'b_o')}
    del _L0_ffn_all
    return {'x': x, 'src': src, 'dst': dst, 'L0_gnn_fc_w': _L0_gnn_in['fc_w'], 'L0_gnn_fc_b': _L0_gnn_in['fc_b'], 'L0_gnn_w1_1': _L0_gnn_in['w1_1'], 'L0_gnn_w2_1': _L0_gnn_in['w2_1'], 'L0_gnn_b_1': _L0_gnn_in['b_1'], 'L0_gnn_w1_2': _L0_gnn_in['w1_2'], 'L0_gnn_w2_2': _L0_gnn_in['w2_2'], 'L0_gnn_b_2': _L0_gnn_in['b_2'], 'L0_ffn_W_f': _L0_ffn_in['W_f'], 'L0_ffn_b_f': _L0_ffn_in['b_f'], 'L0_ffn_W_i': _L0_ffn_in['W_i'], 'L0_ffn_b_i': _L0_ffn_in['b_i'], 'L0_ffn_W_c': _L0_ffn_in['W_c'], 'L0_ffn_b_c': _L0_ffn_in['b_c'], 'L0_ffn_W_o': _L0_ffn_in['W_o'], 'L0_ffn_b_o': _L0_ffn_in['b_o']}

def reference(x, src, dst, L0_gnn_fc_w, L0_gnn_fc_b, L0_gnn_w1_1, L0_gnn_w2_1, L0_gnn_b_1, L0_gnn_w1_2, L0_gnn_w2_2, L0_gnn_b_2, L0_ffn_W_f, L0_ffn_b_f, L0_ffn_W_i, L0_ffn_b_i, L0_ffn_W_c, L0_ffn_b_c, L0_ffn_W_o, L0_ffn_b_o):
    import jax
    import jax.numpy as jnp

    def _L0_gnn_ref(feat, src, dst, fc_w, fc_b, w1_1, w2_1, b_1, w1_2, w2_2, b_2):
        import jax, jax.numpy as jnp
        import numpy as np
        N, E, D_IN, D_H = (2500, 40000, 512, 512)
        ALPHA = 0.1
        LAMBDA = 1.0

        def _gcn2_layer(h, h0, src, dst, norm, w1, w2, b, layer):
            beta = float(np.log(LAMBDA / layer + 1.0))
            x = h * norm
            agg = jax.ops.segment_sum(x[src], dst, num_segments=h.shape[0])
            agg = agg * norm
            f = agg * (1.0 - ALPHA)
            f0 = h0 * ALPHA
            rst = (1.0 - beta) * f + beta * (f @ w1) + (1.0 - beta) * f0 + beta * (f0 @ w2) + b
            return jax.nn.relu(rst)
        n = feat.shape[0]
        h = feat @ fc_w.T + fc_b
        deg = jax.ops.segment_sum(jnp.ones_like(dst, dtype=h.dtype), dst, num_segments=n)
        norm = jnp.clip(deg, 1.0, None) ** (-0.5)
        norm = norm[:, None]
        res = _gcn2_layer(h, h, src, dst, norm, w1_1, w2_1, b_1, layer=1)
        out = _gcn2_layer(res, h, src, dst, norm, w1_2, w2_2, b_2, layer=2)
        return out

    def _L0_ffn_ref(x, W_f, b_f, W_i, b_i, W_c, b_c, W_o, b_o):
        import jax, jax.numpy as jnp
        import numpy as np
        INPUT_SIZE = 512
        HIDDEN_SIZE = 512
        B, T, I = x.shape
        H = W_f.shape[1]
        h0 = jnp.zeros((B, H), dtype=x.dtype)
        c0 = jnp.zeros((B, H), dtype=x.dtype)

        def step(carry, x_t):
            h_prev, c_prev = carry
            combined = jnp.concatenate((x_t, h_prev), axis=1)
            f_t = jax.nn.sigmoid(combined @ W_f + b_f)
            i_t = jax.nn.sigmoid(combined @ W_i + b_i)
            c_tilde = jnp.tanh(combined @ W_c + b_c)
            c_t = f_t * c_prev + i_t * c_tilde
            o_t = jax.nn.sigmoid(combined @ W_o + b_o)
            h_t = o_t * jnp.tanh(c_t)
            return ((h_t, c_t), h_t)
        _, hs = jax.lax.scan(step, (h0, c0), jnp.swapaxes(x, 0, 1))
        return jnp.swapaxes(hs, 0, 1)
    x = x + _L0_gnn_ref(_layernorm(x, axis=-1), src, dst, L0_gnn_fc_w, L0_gnn_fc_b, L0_gnn_w1_1, L0_gnn_w2_1, L0_gnn_b_1, L0_gnn_w1_2, L0_gnn_w2_2, L0_gnn_b_2)
    x = x + _L0_ffn_ref(_layernorm(x, axis=-1)[None], L0_ffn_W_f, L0_ffn_b_f, L0_ffn_W_i, L0_ffn_b_i, L0_ffn_W_c, L0_ffn_b_c, L0_ffn_W_o, L0_ffn_b_o)[0]
    return x

_drawn_inputs = setup_inputs


def setup_inputs(seed=0):
    import zlib

    import numpy as np

    out = dict(_drawn_inputs(seed))
    spreads = {}
    factors = {'L0_gnn_fc_b': 3.595,
     'L0_gnn_w2_1': 5.481,
     'L0_gnn_b_1': 3.331,
     'L0_ffn_W_f': 4.816,
     'L0_ffn_b_f': 64.0,
     'L0_ffn_W_i': 2.897,
     'L0_ffn_b_i': 64.0,
     'L0_ffn_b_c': 7.274,
     'L0_ffn_W_o': 2.81,
     'L0_ffn_b_o': 61.563}
    for name, (base, spread) in spreads.items():
        noise = np.random.default_rng([zlib.crc32(name.encode()), seed]).standard_normal(out[name].shape)
        drawn = base * np.exp(spread * noise) if base else spread * noise
        out[name] = jnp.asarray(drawn.astype(out[name].dtype))
    for name, factor in factors.items():
        out[name] = (out[name] * factor).astype(out[name].dtype)
    return out
```

```python
from contextlib import ExitStack
import math

import concourse.bass as bass
from concourse import mybir

F32 = mybir.dt.float32
BF16 = mybir.dt.bfloat16
I32 = mybir.dt.int32
I16 = mybir.dt.int16
ALU = mybir.AluOpType
ACT = mybir.ActivationFunctionType

P = 128
BANKS = 8
BANK = 512
ALPHA = 0.1
LAMBDA = 1.0
EPS = 1e-5


def gnn_lstm_kernel(nc, x, src, dst, fc_w, fc_b, w1_1, w2_1, b_1, w1_2, w2_2, b_2,
                    W_f, b_f, W_i, b_i, W_c, b_c, W_o, b_o, out):
    N, D = x.shape
    E = src.shape[0]
    K = D // P
    R = 125
    T = N // R
    ET = E // R
    CT = 5
    CHUNKS = ET // CT
    G = 4 * K
    NBLK = [(a, min(BANK, N - a)) for a in range(0, N, BANK)]
    B = len(NBLK)
    assert T * R == N and ET * R == E and CHUNKS * CT == ET and CHUNKS % 2 == 0 and T % 2 == 0

    with ExitStack() as ctx:
        def sb(name, shape, dt=F32):
            return ctx.enter_context(nc.sbuf_tensor(name, shape, dt))

        def sem(name):
            return ctx.enter_context(nc.semaphore(name))

        X_AT = 0
        ROWS_AT = X_AT + T * D
        GW_AT = ROWS_AT + T * D
        A_AT = GW_AT + 6 * K * D
        COL_AT = A_AT + T * N
        END = COL_AT + 3 * K * N
        arena = sb("arena", [P, END])

        def region(at, n, parts=P):
            return arena[0:parts, at:at + n]

        xr = region(X_AT, T * D, R).rearrange("p (t d) -> p t d", t=T)
        rows = region(ROWS_AT, T * D, R).rearrange("p (t d) -> p t d", t=T)
        gw = [region(GW_AT + n * K * D, K * D).rearrange("p (k d) -> p k d", k=K) for n in range(6)]
        fcw, fct, w11, w21, w12, w22 = gw
        adj = region(A_AT, T * N, R).rearrange("p (t n) -> p t n", t=T)
        colA, h0T, aggT = [region(COL_AT + n * K * N, K * N).rearrange("p (k n) -> p k n", k=K)
                           for n in range(3)]
        OH = CT * N // 2
        hot = [[region(COL_AT + (2 * b + s) * OH, OH, R).bitcast(BF16).rearrange("p (t n) -> p t n", t=CT)
                for s in range(2)] for b in range(2)]
        AT = COL_AT + 4 * OH
        iota = region(AT, N // 2, R).bitcast(I16)
        edge_i = [region(AT + N // 2 + s * ET, ET, R).bitcast(I32) for s in range(2)]
        edge_f = [region(AT + N // 2 + (2 + s) * ET, ET, R) for s in range(2)]
        assert AT + N // 2 + 4 * ET <= END
        zT = region(ROWS_AT, G * N).rearrange("p (g n) -> p g n", g=G)
        WX_AT = COL_AT - G * D
        assert ROWS_AT + G * N <= WX_AT
        wx = region(WX_AT, G * D).rearrange("p (k g d) -> p k g d", k=K, g=4)
        wh = region(COL_AT + K * N, G * D).rearrange("p (k g d) -> p k g d", k=K, g=4)
        hT = region(WX_AT, K * N).rearrange("p (k n) -> p k n", k=K)

        ident = sb("ident", [P, P])
        ones = sb("ones", [P, P])
        norm_b = sb("norm_b", [P, N])
        norm_c = sb("norm_c", [P, T])
        bias_r = sb("bias_r", [3 * K + G, P])
        bias = sb("bias", [P, 3 * K + G])
        stats = sb("stats", [P, T, 6])
        mv = sb("mv", [P, T, 2])
        rstd = sb("rstd", [P, T])
        cell = sb("cell", [P, K])
        h_now = sb("h_now", [P, K])
        z_now = sb("z_now", [P, G])
        gates = sb("gates", [P, G])
        ig = sb("ig", [P, K])
        fc = sb("fc", [P, K])
        tc = sb("tc", [P, K])
        ps = ctx.enter_context(nc.psum_tensor("ps", [P, BANKS, BANK], F32))

        edges_in = sem("edges_in")
        x_in = sem("x_in")
        w_in = sem("w_in")
        bias_in = sem("bias_in")
        wx_in = sem("wx_in")
        wh_in = sem("wh_in")
        stored = sem("stored")
        consts = sem("consts")
        edges_f = sem("edges_f")
        hot_ready = sem("hot_ready")
        counted = sem("counted")
        added = sem("added")
        filled = [sem(f"filled{b}") for b in range(BANKS)]
        emptied = [sem(f"emptied{b}") for b in range(BANKS)]
        chained = sem("chained")
        stat_ready = sem("stat_ready")
        var_ready = sem("var_ready")
        std_ready = sem("std_ready")
        root_ready = sem("root_ready")
        norm_ready = sem("norm_ready")
        cell_step = sem("cell_step")
        hT_ready = sem("hT_ready")
        folded = sem("folded")
        h_ready = sem("h_ready")
        gates_ready = sem("gates_ready")
        z_ready = sem("z_ready")
        act_ready = sem("act_ready")
        c_ready = sem("c_ready")
        tc_ready = sem("tc_ready")
        ln_rows = sem("ln_rows")

        counts = {"bias": 1, "fct": K, "deg": B, "xT": T, "norm": 1, "h0": K * B, "h0r": T,
                  "agg1": K * B, "res1": K * B, "res1r": T, "agg2": K * B, "res2": K * B,
                  "res2r": T, "x2T": T, "z": G * B, "out": T}
        first, at = {}, 0
        for name, c in counts.items():
            first[name] = at
            at += c

        def bank(stage, i):
            return ps[:, (first[stage] + i) % BANKS, :]

        def wait_filled(eng, stage, i):
            n = first[stage] + i
            eng.wait_ge(filled[n % BANKS], n // BANKS + 1)

        def wait_emptied(eng, stage, i):
            n = first[stage] + i
            eng.wait_ge(emptied[n % BANKS], n // BANKS + 1)

        def wait_bank(eng, stage, i):
            n = first[stage] + i
            if n >= BANKS:
                eng.wait_ge(emptied[n % BANKS], n // BANKS)

        def fill(ins, stage, i):
            ins.then_inc(filled[(first[stage] + i) % BANKS], 1)

        def empty(ins, stage, i):
            ins.then_inc(emptied[(first[stage] + i) % BANKS], 1)

        block = ctx.enter_context(nc.Block())

        @block.sync
        def _(sp):
            for s, e in ((0, src), (1, dst)):
                sp.dma_start(edge_i[s], e.rearrange("(p t) -> p t", p=R)).then_inc(edges_in, 16)
            sp.dma_start(xr, x.rearrange("(t p) d -> p t d", p=R)).then_inc(x_in, 16)
            at = 0
            for b in (fc_b, b_1, b_2, b_f, b_i, b_o, b_c):
                sp.dma_start(bias_r[at:at + K, :], b.rearrange("(k p) -> k p", p=P)).then_inc(bias_in, 16)
                at += K
            for to, w in ((fcw, fc_w), (w11, w1_1), (w21, w2_1), (w12, w1_2), (w22, w2_2)):
                sp.dma_start(to, w.rearrange("(k p) d -> p k d", p=P)).then_inc(w_in, 16)
            for i in range(K * B - BANKS, K * B):
                wait_emptied(sp, "agg2", i)
            for g, w in enumerate((W_f, W_i, W_o, W_c)):
                sp.dma_start(wx[:, :, g, :], w[0:D, :].rearrange("(k p) d -> p k d", p=P)).then_inc(wx_in, 16)
            for i in range(K * B - BANKS, K * B):
                wait_emptied(sp, "res2", i)
            for g, w in enumerate((W_f, W_i, W_o, W_c)):
                sp.dma_start(wh[:, :, g, :], w[D:2 * D, :].rearrange("(k p) d -> p k d", p=P)).then_inc(wh_in, 16)
            out_v = out.rearrange("(t p) d -> p t d", p=R)
            for t in range(T):
                wait_emptied(sp, "out", t)
                sp.dma_start(out_v[:, t, :], xr[:, t, :]).then_inc(stored, 16)
            sp.wait_ge(stored, 16 * T)

        @block.gpsimd
        def _(pool):
            nc.gpsimd.iota(iota, [[1, N]], base=0, channel_multiplier=0).then_inc(consts, 1)
            nc.gpsimd.memset(ident[:, :], 0.0).then_inc(consts, 1)
            nc.gpsimd.memset(ones[:, :], 1.0).then_inc(consts, 1)
            pool.wait_ge(consts, 3)
            nc.gpsimd.affine_select(out=ident[:, :], in_=ident[:, :], compare_op=ALU.not_equal, fill=1.0,
                                    base=0, pattern=[[-1, P]], channel_multiplier=1).then_inc(consts, 1)

        @block.tensor
        def _(pe):
            def count_chunk(c, b):
                with pe.Fori(0, T // 2) as mp:
                    for half in range(2):
                        m = mp * 2 + half
                        pe.wait_ge(hot_ready, c + 1)
                        pe.wait_ge(added, c * T + m + 1)
                        for t in range(CT):
                            for n, (a, w) in enumerate(NBLK):
                                mm = nc.tensor.matmul(ps[0:R, B * half + n, 0:w],
                                                      hot[b][0][:, t, bass.ds(m * R, R)],
                                                      hot[b][1][:, t, a:a + w],
                                                      start=(t == 0), stop=(t == CT - 1))
                        mm.then_inc(counted, 1)

            with pe.Fori(0, CHUNKS // 2) as cp:
                count_chunk(cp * 2, 0)
                count_chunk(cp * 2 + 1, 1)

            pe.wait_ge(consts, 4)
            pe.wait_ge(added, CHUNKS * T + 2)
            pe.wait_ge(bias_in, 16 * 7)
            fill(nc.tensor.transpose(bank("bias", 0)[:, 0:3 * K + G], bias_r[:, :], ident[0:3 * K + G, 0:3 * K + G]),
                 "bias", 0)
            pe.wait_ge(w_in, 16 * 5)
            for o in range(K):
                for i in range(K):
                    mm = nc.tensor.transpose(bank("fct", o)[:, i * P:(i + 1) * P], fcw[:, o, i * P:(i + 1) * P],
                                             ident[:, :])
                fill(mm, "fct", o)
            for n, (a, w) in enumerate(NBLK):
                wait_bank(pe, "deg", n)
                for s in range(T):
                    mm = nc.tensor.matmul(bank("deg", n)[:, 0:w], ones[0:R, :], adj[:, s, a:a + w],
                                          start=(s == 0), stop=(s == T - 1))
                fill(mm, "deg", n)

            def to_columns(stage):
                for t in range(T):
                    wait_bank(pe, stage, t)
                    for k in range(K):
                        mm = nc.tensor.transpose(bank(stage, t)[:, k * R:(k + 1) * R],
                                                 rows[:, t, k * P:(k + 1) * P], ident[0:R, 0:R])
                    fill(mm, stage, t)

            def to_rows(stage, cols, ready):
                for i in ready:
                    wait_emptied(pe, *i)
                for t in range(T):
                    wait_bank(pe, stage, t)
                    for k in range(K):
                        mm = nc.tensor.transpose(bank(stage, t)[0:R, k * P:(k + 1) * P],
                                                 cols[:, k, t * R:(t + 1) * R], ident[:, :])
                    fill(mm, stage, t)

            def dense(stage, pairs):
                for f in range(K):
                    for n, (a, w) in enumerate(NBLK):
                        wait_bank(pe, stage, f * B + n)
                        for j, (wt, cols) in enumerate(pairs):
                            for k in range(K):
                                mm = nc.tensor.matmul(bank(stage, f * B + n)[:, 0:w], wt[:, k, f * P:(f + 1) * P],
                                                      cols[:, k, a:a + w], start=(j + k == 0),
                                                      stop=(j == len(pairs) - 1 and k == K - 1))
                        fill(mm, stage, f * B + n)

            def gather(stage, before):
                for f in range(K):
                    for n, (a, w) in enumerate(NBLK):
                        wait_bank(pe, stage, f * B + n)
                        for s in range(T):
                            if f + n == 0:
                                wait_emptied(pe, before, s)
                            mm = nc.tensor.matmul(bank(stage, f * B + n)[:, 0:w], rows[:, s, f * P:(f + 1) * P],
                                                  adj[:, s, a:a + w], start=(s == 0), stop=(s == T - 1))
                        fill(mm, stage, f * B + n)

            pe.wait_ge(ln_rows, T)
            to_columns("xT")
            wait_bank(pe, "norm", 0)
            pe.wait_ge(norm_ready, 1)
            for t in range(T):
                mm = nc.tensor.transpose(bank("norm", 0)[0:R, t:t + 1], norm_b[0:1, t * R:(t + 1) * R],
                                         ident[0:1, 0:1])
            fill(mm, "norm", 0)
            for t in range(T):
                wait_emptied(pe, "xT", t)
            dense("h0", [(fct, colA)])
            to_rows("h0r", h0T, [("h0", i) for i in range(K * B)])
            gather("agg1", "h0r")
            pe.wait_ge(folded, 4 * (1 + K))
            for i in range(K * B):
                wait_emptied(pe, "agg1", i)
            dense("res1", [(w11, aggT), (w21, h0T)])
            to_rows("res1r", colA, [("res1", i) for i in range(K * B)])
            gather("agg2", "res1r")
            for i in range(K * B):
                wait_emptied(pe, "agg2", i)
            dense("res2", [(w12, aggT), (w22, h0T)])
            to_rows("res2r", colA, [("res2", i) for i in range(K * B)])
            pe.wait_ge(ln_rows, 2 * T)
            to_columns("x2T")
            pe.wait_ge(wx_in, 16 * 4)
            for t in range(T):
                wait_emptied(pe, "x2T", t)
            for g in range(G):
                for n, (a, w) in enumerate(NBLK):
                    wait_bank(pe, "z", g * B + n)
                    for k in range(K):
                        mm = nc.tensor.matmul(bank("z", g * B + n)[:, 0:w],
                                              wx[:, k, g // K, (g % K) * P:(g % K + 1) * P],
                                              colA[:, k, a:a + w], start=(k == 0), stop=(k == K - 1))
                    fill(mm, "z", g * B + n)
            pe.wait_ge(wh_in, 16 * 4)
            for i in range(G * B - BANKS, G * B):
                wait_emptied(pe, "z", i)
            with pe.Fori(0, N) as t:
                pe.wait_ge(h_ready, t + 2)
                for g in range(G):
                    for k in range(K):
                        mm = nc.tensor.matmul(ps[:, 0, g:g + 1], wh[:, k, g // K, (g % K) * P:(g % K + 1) * P],
                                              h_now[:, k:k + 1], start=(k == 0), stop=(k == K - 1))
                mm.then_inc(gates_ready, 1)
            pe.wait_ge(hT_ready, N)
            to_rows("out", hT, [])

        @block.scalar
        def _(act):
            def roots(n):
                act.wait_ge(var_ready, n)
                nc.scalar.activation(rstd[0:R, :], rstd[0:R, :], ACT.Sqrt).then_inc(std_ready, 1)

            def columns_out(stage, to, func, b):
                for f in range(K):
                    for n, (a, w) in enumerate(NBLK):
                        wait_filled(act, stage, f * B + n)
                        empty(nc.scalar.activation(to[:, f, a:a + w], bank(stage, f * B + n)[:, 0:w], func,
                                                   bias=bias[:, b + f:b + f + 1]), stage, f * B + n)

            roots(1)
            for n in range(B):
                wait_emptied(act, "deg", n)
            nc.scalar.activation(norm_b[:, :], norm_b[:, :], ACT.Sqrt).then_inc(root_ready, 1)
            wait_emptied(act, "bias", 0)
            columns_out("h0", h0T, ACT.Identity, 0)
            columns_out("res1", colA, ACT.Relu, K)
            columns_out("res2", colA, ACT.Relu, 2 * K)
            roots(2)
            for t in range(T):
                wait_filled(act, "x2T", t)
                empty(nc.scalar.copy(colA[:, :, t * R:(t + 1) * R],
                                     bank("x2T", t)[:, 0:K * R].rearrange("p (k r) -> p k r", k=K)), "x2T", t)
            for g in range(0, G, 2):
                for n, (a, w) in enumerate(NBLK):
                    wait_filled(act, "z", g * B + n)
                    empty(nc.scalar.activation(zT[:, g, a:a + w], bank("z", g * B + n)[:, 0:w], ACT.Identity,
                                               bias=bias[:, 3 * K + g:3 * K + g + 1]), "z", g * B + n)
            with act.Fori(0, N) as t:
                act.wait_ge(z_ready, t + 1)
                nc.scalar.activation(gates[:, 0:3 * K], z_now[:, 0:3 * K], ACT.Sigmoid).then_inc(act_ready, 1)
                nc.scalar.activation(gates[:, 3 * K:G], z_now[:, 3 * K:G], ACT.Tanh).then_inc(act_ready, 1)
                act.wait_ge(c_ready, t + 1)
                nc.scalar.activation(tc[:, :], cell[:, :], ACT.Tanh).then_inc(tc_ready, 1)

        @block.vector
        def _(dve):
            link_n = [0]

            def link(ins):
                link_n[0] += 1
                ins.then_inc(chained, 1)
                dve.wait_ge(chained, link_n[0])

            def hot_rows(c, b):
                for s in range(2):
                    for t in range(CT):
                        ins = nc.vector.tensor_scalar(hot[b][s][:, t, :], iota,
                                                      edge_f[s][:, bass.ds(c * CT + t, 1)], None, ALU.is_equal)
                ins.then_inc(hot_ready, 1)

            def add_counts(c):
                with dve.Fori(0, T // 2) as mp:
                    for half in range(2):
                        m = mp * 2 + half
                        dve.wait_ge(counted, c * T + m + 1)
                        to = adj[:, bass.ds(m, 1), :].rearrange("p o n -> p (o n)")
                        got = ps[0:R, B * half:B * half + B, :].rearrange("p b n -> p (b n)")[:, 0:N]
                        nc.vector.tensor_tensor(to, to, got, ALU.add).then_inc(added, 1)

            def normalize(n):
                for t in range(T):
                    nc.vector.bn_stats(stats[0:R, t, :], xr[:, t, :]).then_inc(stat_ready, 1)
                dve.wait_ge(stat_ready, T * n)
                for t in range(T):
                    ins = nc.vector.bn_aggr(mv[0:R, t, :], stats[0:R, t, :])
                link(ins)
                nc.vector.tensor_scalar(rstd[0:R, :], mv[0:R, :, 1], EPS, None, ALU.add).then_inc(var_ready, 1)
                dve.wait_ge(std_ready, n)
                link(nc.vector.reciprocal(rstd[0:R, :], rstd[0:R, :]))
                for t in range(T):
                    nc.vector.tensor_scalar(rows[:, t, :], xr[:, t, :], mv[0:R, t, 0:1], rstd[0:R, t:t + 1],
                                            ALU.subtract, ALU.mult).then_inc(ln_rows, 1)

            def rows_out(stage):
                for t in range(T):
                    wait_filled(dve, stage, t)
                    empty(nc.vector.tensor_scalar(rows[:, t, :], bank(stage, t)[0:R, :], norm_c[0:R, t:t + 1],
                                                  None, ALU.mult), stage, t)

            def sums_out(stage):
                for f in range(K):
                    for n, (a, w) in enumerate(NBLK):
                        wait_filled(dve, stage, f * B + n)
                        empty(nc.vector.scalar_tensor_tensor(
                            out=aggT[:, f, a:a + w], in0=bank(stage, f * B + n)[:, 0:w], scalar=1.0 - ALPHA,
                            in1=norm_b[:, a:a + w], op0=ALU.mult, op1=ALU.mult), stage, f * B + n)

            dve.wait_ge(edges_in, 32)
            for s in range(2):
                nc.vector.tensor_copy(edge_f[s], edge_i[s]).then_inc(edges_f, 1)
            for s in range(2):
                nc.vector.memset(adj[:, s * T // 2:(s + 1) * T // 2, :], 0.0).then_inc(added, 1)
            dve.wait_ge(consts, 3)
            dve.wait_ge(edges_f, 2)
            hot_rows(0, 0)
            dve.wait_ge(x_in, 16)
            normalize(1)
            dve.wait_ge(added, 2)
            with dve.Fori(0, CHUNKS // 2 - 1) as cp:
                hot_rows(cp * 2 + 1, 1)
                add_counts(cp * 2)
                hot_rows(cp * 2 + 2, 0)
                add_counts(cp * 2 + 1)
            hot_rows(CHUNKS - 1, 1)
            add_counts(CHUNKS - 2)
            add_counts(CHUNKS - 1)

            wait_filled(dve, "bias", 0)
            empty(nc.vector.tensor_copy(bias[:, :], bank("bias", 0)[:, 0:3 * K + G]), "bias", 0)
            for o in range(K):
                wait_filled(dve, "fct", o)
                empty(nc.vector.tensor_copy(fct[:, :, o * P:(o + 1) * P],
                                            bank("fct", o).rearrange("p (k d) -> p k d", k=K)), "fct", o)
            for n, (a, w) in enumerate(NBLK):
                wait_filled(dve, "deg", n)
                empty(nc.vector.tensor_scalar(norm_b[:, a:a + w], bank("deg", n)[:, 0:w], 1.0, None, ALU.max),
                      "deg", n)
            dve.wait_ge(root_ready, 1)
            nc.vector.reciprocal(norm_b[:, :], norm_b[:, :]).then_inc(norm_ready, 1)
            for t in range(T):
                wait_filled(dve, "xT", t)
                empty(nc.vector.tensor_copy(colA[:, :, t * R:(t + 1) * R],
                                            bank("xT", t)[:, 0:K * R].rearrange("p (k r) -> p k r", k=K)), "xT", t)
            wait_filled(dve, "norm", 0)
            ins = nc.vector.tensor_copy(norm_c[0:R, :], bank("norm", 0)[0:R, 0:T])
            empty(ins, "norm", 0)
            wait_emptied(dve, "norm", 0)
            dve.wait_ge(w_in, 16 * 5)
            n = 0
            for layer, pair in ((1, (w11, w21)), (2, (w12, w22))):
                beta = math.log(LAMBDA / layer + 1.0)
                for w, c in zip(pair, (1.0, ALPHA)):
                    nc.vector.tensor_scalar(w, w, c * beta, None, ALU.mult).then_inc(folded, 1)
                    n += 1
                    dve.wait_ge(folded, n)
                    for k in range(K):
                        d = w[:, k, k * P:(k + 1) * P]
                        nc.vector.scalar_tensor_tensor(out=d, in0=ident[:, :], scalar=c * (1.0 - beta), in1=d,
                                                       op0=ALU.mult, op1=ALU.add).then_inc(folded, 1)
                        n += 1
            dve.wait_ge(norm_ready, 1)
            rows_out("h0r")
            sums_out("agg1")
            rows_out("res1r")
            sums_out("agg2")
            for t in range(T):
                wait_filled(dve, "res2r", t)
                empty(nc.vector.tensor_tensor(xr[:, t, :], xr[:, t, :], bank("res2r", t)[0:R, :], ALU.add),
                      "res2r", t)
            for t in range(T):
                wait_emptied(dve, "res2r", t)
            normalize(2)
            for g in range(1, G, 2):
                for n, (a, w) in enumerate(NBLK):
                    wait_filled(dve, "z", g * B + n)
                    empty(nc.vector.tensor_scalar(zT[:, g, a:a + w], bank("z", g * B + n)[:, 0:w],
                                                  bias[:, 3 * K + g:3 * K + g + 1], None, ALU.add),
                          "z", g * B + n)
            nc.vector.memset(cell[:, :], 0.0).then_inc(h_ready, 1)
            nc.vector.memset(h_now[:, :], 0.0).then_inc(h_ready, 1)
            dve.wait_ge(h_ready, 2)
            for i in range(G * B - BANKS, G * B):
                wait_emptied(dve, "z", i)
            with dve.Fori(0, N) as t:
                dve.wait_ge(gates_ready, t + 1)
                z_t = zT[:, :, bass.ds(t, 1)].rearrange("p g o -> p (g o)")
                nc.vector.tensor_tensor(z_now[:, :], z_t, ps[:, 0, 0:G], ALU.add).then_inc(z_ready, 1)
                dve.wait_ge(act_ready, t * 2 + 2)
                nc.vector.tensor_tensor(ig[:, :], gates[:, K:2 * K], gates[:, 3 * K:G], ALU.mult).then_inc(cell_step, 1)
                nc.vector.tensor_tensor(fc[:, :], gates[:, 0:K], cell[:, :], ALU.mult).then_inc(cell_step, 1)
                dve.wait_ge(cell_step, t * 2 + 2)
                nc.vector.tensor_tensor(cell[:, :], ig[:, :], fc[:, :], ALU.add).then_inc(c_ready, 1)
                dve.wait_ge(tc_ready, t + 1)
                dve.wait_ge(c_ready, t + 1)
                nc.vector.tensor_tensor(h_now[:, :], gates[:, 2 * K:3 * K], tc[:, :], ALU.mult).then_inc(h_ready, 1)
                h_t = hT[:, :, bass.ds(t, 1)].rearrange("p k o -> p (k o)")
                nc.vector.tensor_tensor(h_t, gates[:, 2 * K:3 * K], tc[:, :], ALU.mult).then_inc(hT_ready, 1)
            for t in range(T):
                wait_filled(dve, "out", t)
                empty(nc.vector.tensor_tensor(xr[:, t, :], xr[:, t, :], bank("out", t)[0:R, :], ALU.add), "out", t)


_INS = ["x", "src", "dst", "L0_gnn_fc_w", "L0_gnn_fc_b", "L0_gnn_w1_1", "L0_gnn_w2_1", "L0_gnn_b_1",
        "L0_gnn_w1_2", "L0_gnn_w2_2", "L0_gnn_b_2", "L0_ffn_W_f", "L0_ffn_b_f", "L0_ffn_W_i", "L0_ffn_b_i",
        "L0_ffn_W_c", "L0_ffn_b_c", "L0_ffn_W_o", "L0_ffn_b_o"]


def kernel(**inputs):
    import numpy as np
    import concourse.bacc as bacc
    from concourse import mybir as mb
    from concourse.bass_utils import run_bass_kernel_spmd

    nc = bacc.Bacc("TRN2", target_bir_lowering=False, num_devices=1)
    arrays, args = {}, []
    for name in _INS:
        a = np.ascontiguousarray(inputs[name])
        arrays[f"in_{name}"] = a
        args.append(nc.dram_tensor(f"in_{name}", a.shape, mb.dt.from_np(a.dtype), kind="ExternalInput").ap())
    out = nc.dram_tensor("out_0", inputs["x"].shape, mb.dt.float32, kind="ExternalOutput").ap()
    gnn_lstm_kernel(nc, *args, out)
    return run_bass_kernel_spmd(nc, [arrays], core_ids=[0]).results[0]["out_0"]
```

```python
from contextlib import ExitStack
import math

import concourse.bass as bass
from concourse import mybir

F32 = mybir.dt.float32
BF16 = mybir.dt.bfloat16
I32 = mybir.dt.int32
I16 = mybir.dt.int16
ALU = mybir.AluOpType
ACT = mybir.ActivationFunctionType
AX = mybir.AxisListType

P = 128
BANKS = 8
BANK = 512
ALPHA = 0.1
LAMBDA = 1.0
EPS = 1e-5


def gnn_lstm_kernel(nc, x, src, dst, fc_w, fc_b, w1_1, w2_1, b_1, w1_2, w2_2, b_2,
                    W_f, b_f, W_i, b_i, W_c, b_c, W_o, b_o, out):
    N, D = x.shape
    E = src.shape[0]
    K = D // P
    R = 125
    T = N // R
    ET = E // R
    CT = 5
    CHUNKS = ET // CT
    G = 4 * K
    NBLK = [(a, min(BANK, N - a)) for a in range(0, N, BANK)]
    B = len(NBLK)
    assert T * R == N and ET * R == E and CHUNKS * CT == ET and CHUNKS % 2 == 0 and T % 2 == 0

    with ExitStack() as ctx:
        def sb(name, shape, dt=F32):
            return ctx.enter_context(nc.sbuf_tensor(name, shape, dt))

        def sem(name):
            return ctx.enter_context(nc.semaphore(name))

        X_AT = 0
        ROWS_AT = X_AT + T * D
        GW_AT = ROWS_AT + T * D
        A_AT = GW_AT + 6 * K * D
        COL_AT = A_AT + T * N
        NORM_AT = COL_AT + 3 * K * N
        HALF = K * G * P // 2
        W_AT = COL_AT + K * N
        END = W_AT + 3 * HALF
        assert NORM_AT + N <= END
        arena = sb("arena", [P, END])

        def region(at, n, parts=P):
            return arena[0:parts, at:at + n]

        xr = region(X_AT, T * D, R).rearrange("p (t d) -> p t d", t=T)
        rows = region(ROWS_AT, T * D, R).rearrange("p (t d) -> p t d", t=T)
        gw = [region(GW_AT + n * K * D, K * D).rearrange("p (k d) -> p k d", k=K) for n in range(6)]
        fcw, fct, w11, w21, w12, w22 = gw
        adj = region(A_AT, T * N, R).rearrange("p (t n) -> p t n", t=T)
        colA, h0T, aggT = [region(COL_AT + n * K * N, K * N).rearrange("p (k n) -> p k n", k=K)
                           for n in range(3)]
        OH = CT * N // 2
        hot = [[region(COL_AT + (2 * b + s) * OH, OH, R).bitcast(BF16).rearrange("p (t n) -> p t n", t=CT)
                for s in range(2)] for b in range(2)]
        AT = COL_AT + 4 * OH
        iota = region(AT, N // 2, R).bitcast(I16)
        edge_i = [region(AT + N // 2 + s * ET, ET, R).bitcast(I32) for s in range(2)]
        edge_f = [region(AT + N // 2 + (2 + s) * ET, ET, R) for s in range(2)]
        assert AT + N // 2 + 4 * ET <= NORM_AT
        zT = region(ROWS_AT, G * N).rearrange("p (g n) -> p g n", g=G)
        WX_AT = COL_AT - G * D
        assert ROWS_AT + G * N <= WX_AT
        wx = region(WX_AT, G * D).rearrange("p (k g d) -> p k g d", k=K, g=4)
        w_part = [region(W_AT + n * HALF, HALF).bitcast(BF16).rearrange("p (k g d) -> p k g d", k=K, g=4)
                  for n in range(3)]
        SPLIT_AT = ROWS_AT + G * N
        SLOTS = 3
        assert SPLIT_AT + SLOTS * D <= WX_AT
        split = [region(SPLIT_AT + n * D, D) for n in range(SLOTS)]
        WIN = 418
        WINS = [(a, min(WIN, N - a) if a == 0 else 416) for a in (0, 418, 834)]
        assert sum(w for _, w in WINS) == N
        Q = len(WINS)
        U = Q * K
        OPN = K * (N + 2) // 2
        LIVE = 3
        gates_at = SPLIT_AT + 3 * OPN
        cells_at = gates_at + LIVE * 4 * WIN
        assert cells_at + K * WIN <= W_AT
        spots = [SPLIT_AT, SPLIT_AT + OPN, SPLIT_AT + 2 * OPN, END - OPN]
        oper = [region(o, OPN).bitcast(BF16).rearrange("p (k n) -> p k n", k=K) for o in spots]
        gate = [region(gates_at + n * 4 * WIN, 4 * WIN).rearrange("p (g n) -> p g n", g=4) for n in range(LIVE)]
        cells = region(cells_at, K * WIN).rearrange("p (k n) -> p k n", k=K)
        hT = region(W_AT + HALF, K * N).rearrange("p (k n) -> p k n", k=K)
        assert W_AT + HALF + K * N <= END - OPN
        z4 = zT.rearrange("p (g k) n -> p g k n", g=4)
        wh = region(SPLIT_AT, G * D).rearrange("p (k g d) -> p k g d", k=K, g=4)
        norm_b = region(NORM_AT, N)
        zx_kept = nc.dram_tensor("zx_kept", [P, G * N], F32).ap()

        ident = sb("ident", [P, P])
        ones = sb("ones", [P, P])
        norm_c = sb("norm_c", [P, T])
        bias_r = sb("bias_r", [3 * K + G, P])
        bias = sb("bias", [P, 3 * K + G])
        stats = sb("stats", [P, T, 6])
        mv = sb("mv", [P, T, 2])
        rstd = sb("rstd", [P, T])
        cell = sb("cell", [P, K])
        h_now = sb("h_now", [P, K])
        z_now = sb("z_now", [P, G])
        gates = sb("gates", [P, G])
        ig = sb("ig", [P, K])
        fc = sb("fc", [P, K])
        tc = sb("tc", [P, K])
        change = sb("change", [P, 2, U])
        worst = sb("worst", [P, 2])
        far = sb("far", [1, 1])
        flag = sb("flag", [1, 1], I32)
        ps = ctx.enter_context(nc.psum_tensor("ps", [P, BANKS, BANK], F32))

        edges_in = sem("edges_in")
        x_in = sem("x_in")
        w_in = sem("w_in")
        bias_in = sem("bias_in")
        wx_in = sem("wx_in")
        wh_in = sem("wh_in")
        stored = sem("stored")
        consts = sem("consts")
        edges_f = sem("edges_f")
        hot_ready = sem("hot_ready")
        counted = sem("counted")
        added = sem("added")
        filled = [sem(f"filled{b}") for b in range(BANKS)]
        emptied = [sem(f"emptied{b}") for b in range(BANKS)]
        chained = sem("chained")
        stat_ready = sem("stat_ready")
        var_ready = sem("var_ready")
        std_ready = sem("std_ready")
        root_ready = sem("root_ready")
        norm_ready = sem("norm_ready")
        cell_step = sem("cell_step")
        hT_ready = sem("hT_ready")
        folded = sem("folded")
        h_ready = sem("h_ready")
        gates_ready = sem("gates_ready")
        z_ready = sem("z_ready")
        act_ready = sem("act_ready")
        c_ready = sem("c_ready")
        tc_ready = sem("tc_ready")
        ln_rows = sem("ln_rows")
        piece_in = [sem(f"piece_in{n}") for n in range(SLOTS)]
        high_ready = sem("high_ready")
        rest_ready = sem("rest_ready")
        mid_ready = sem("mid_ready")
        low_ready = sem("low_ready")
        zx_saved = sem("zx_saved")
        zx_back = sem("zx_back")
        started = sem("started")
        unit_summed = sem("unit_summed")
        z_added = sem("z_added")
        unit_gated = sem("unit_gated")
        ig_ready = sem("ig_ready")
        cells_ready = sem("cells_ready")
        tanh_ready = sem("tanh_ready")
        hidden_ready = sem("hidden_ready")
        oper_ready = sem("oper_ready")
        diff_step = sem("diff_step")
        worst_ready = sem("worst_ready")
        worst_turned = sem("worst_turned")
        flag_ready = sem("flag_ready")

        counts = {"bias": 1, "fct": K, "deg": B, "xT": T, "norm": 1, "h0": K * B, "h0r": T,
                  "agg1": K * B, "res1": K * B, "res1r": T, "agg2": K * B, "res2": K * B,
                  "res2r": T, "x2T": T, "z": G * B, "out": T}
        first, at = {}, 0
        for name, c in counts.items():
            first[name] = at
            at += c

        def bank(stage, i):
            return ps[:, (first[stage] + i) % BANKS, :]

        def wait_filled(eng, stage, i):
            n = first[stage] + i
            eng.wait_ge(filled[n % BANKS], n // BANKS + 1)

        def wait_emptied(eng, stage, i):
            n = first[stage] + i
            eng.wait_ge(emptied[n % BANKS], n // BANKS + 1)

        def wait_bank(eng, stage, i):
            n = first[stage] + i
            if n >= BANKS:
                eng.wait_ge(emptied[n % BANKS], n // BANKS)

        def fill(ins, stage, i):
            ins.then_inc(filled[(first[stage] + i) % BANKS], 1)

        def empty(ins, stage, i):
            ins.then_inc(emptied[(first[stage] + i) % BANKS], 1)

        REST_LIMIT = 2.0 ** -6
        CHANGE_LIMIT = 2.0 ** -16

        class Sweep:
            def __init__(self, source, parts, keep, taken, to):
                self.source = source
                self.parts = parts
                self.keep = keep
                self.taken = taken
                self.to = to

        A, D_, E_ = 0, 1, 3

        def all_sweeps(eng, sweep, before=None):
            before = before or {}
            sweep(0, Sweep(None, (), False, (), 0))
            with eng.Fori(0, 2) as r:
                sweep(r * 2 + 1, Sweep(0, (0,), False, (), 1))
                sweep(r * 2 + 2, Sweep(1, (0,), False, (), 0))
            before.get(5, lambda: None)()
            sweep(5, Sweep(A, (0, 1, 2), True, (A,), 1))
            with eng.Fori(0, 2) as r:
                sweep(r * 2 + 6, Sweep(1, (0,), False, (A,), 2))
                sweep(r * 2 + 7, Sweep(2, (0,), False, (A,), 1))
            sweep(10, Sweep(D_, (0, 1), True, (A, D_), 2))
            before.get(11, lambda: None)()
            sweep(11, Sweep(2, (0,), False, (A, D_), E_))
            sweep(12, Sweep(E_, (0,), False, (A, D_, E_), None))

        block = ctx.enter_context(nc.Block())

        @block.sync
        def _(sp):
            for s, e in ((0, src), (1, dst)):
                sp.dma_start(edge_i[s], e.rearrange("(p t) -> p t", p=R)).then_inc(edges_in, 16)
            sp.dma_start(xr, x.rearrange("(t p) d -> p t d", p=R)).then_inc(x_in, 16)
            at = 0
            for b in (fc_b, b_1, b_2, b_f, b_i, b_o, b_c):
                sp.dma_start(bias_r[at:at + K, :], b.rearrange("(k p) -> k p", p=P)).then_inc(bias_in, 16)
                at += K
            for to, w in ((fcw, fc_w), (w11, w1_1), (w21, w2_1), (w12, w1_2), (w22, w2_2)):
                sp.dma_start(to, w.rearrange("(k p) d -> p k d", p=P)).then_inc(w_in, 16)
            for i in range(K * B - BANKS, K * B):
                wait_emptied(sp, "agg2", i)
            for g, w in enumerate((W_f, W_i, W_o, W_c)):
                sp.dma_start(wx[:, :, g, :], w[0:D, :].rearrange("(k p) d -> p k d", p=P)).then_inc(wx_in, 16)
            for i in range(K * B - BANKS, K * B):
                wait_emptied(sp, "res2", i)
            for n in range(K * 4):
                k, g = n // 4, n % 4
                if n >= SLOTS:
                    sp.wait_ge(low_ready, n - SLOTS + 1)
                sp.dma_start(split[n % SLOTS], (W_f, W_i, W_o, W_c)[g][D + k * P:D + (k + 1) * P, :])\
                    .then_inc(piece_in[n % SLOTS], 16)
            for i in range(G * B - BANKS, G * B):
                wait_emptied(sp, "z", i)
            sp.dma_start(zx_kept, region(ROWS_AT, G * N)).then_inc(zx_saved, 16)
            sp.wait_ge(zx_saved, 16)
            sp.wait_ge(flag_ready, 1)
            with sp.If(sp.value_load(flag[0:1, 0:1], min_val=0, max_val=1) != 0):
                sp.dma_start(region(ROWS_AT, G * N), zx_kept).then_inc(zx_back, 16)
                for g, w in enumerate((W_f, W_i, W_o, W_c)):
                    sp.dma_start(wh[:, :, g, :], w[D:2 * D, :].rearrange("(k p) d -> p k d", p=P)).then_inc(wh_in, 16)
            out_v = out.rearrange("(t p) d -> p t d", p=R)
            for t in range(T):
                wait_emptied(sp, "out", t)
                sp.dma_start(out_v[:, t, :], xr[:, t, :]).then_inc(stored, 16)
            sp.wait_ge(stored, 16 * T)

        @block.gpsimd
        def _(pool):
            nc.gpsimd.iota(iota, [[1, N]], base=0, channel_multiplier=0).then_inc(consts, 1)
            nc.gpsimd.memset(ident[:, :], 0.0).then_inc(consts, 1)
            nc.gpsimd.memset(ones[:, :], 1.0).then_inc(consts, 1)
            pool.wait_ge(consts, 3)
            nc.gpsimd.affine_select(out=ident[:, :], in_=ident[:, :], compare_op=ALU.not_equal, fill=1.0,
                                    base=0, pattern=[[-1, P]], channel_multiplier=1).then_inc(consts, 1)

            def sweep(s, sw):
                for i in range(U + 1):
                    if i < U:
                        g = gate[i % LIVE][:, :, 0:WINS[i // K][1]]
                        pool.wait_ge(unit_gated, s * (2 * U) + (2 * i + 2))
                        nc.gpsimd.tensor_tensor(g[:, 1, :], g[:, 1, :], g[:, 3, :], ALU.mult).then_inc(ig_ready, 1)
                    if i >= 1:
                        a, w = WINS[(i - 1) // K]
                        j = (i - 1) % K
                        g = gate[(i - 1) % LIVE][:, :, 0:w]
                        pool.wait_ge(tanh_ready, s * U + i)
                        if sw.to is None:
                            h, done = hT[:, j, a:a + w], hidden_ready
                        elif sw.taken:
                            h, done = g[:, 2, :], hidden_ready
                        else:
                            h, done = oper[sw.to][:, j, 1 + a:1 + a + w], oper_ready
                        nc.gpsimd.tensor_tensor(h, g[:, 2, :], g[:, 3, :], ALU.mult).then_inc(done, 1)

            pool.wait_ge(started, 3)
            all_sweeps(pool, sweep)

        @block.tensor
        def _(pe):
            def count_chunk(c, b):
                with pe.Fori(0, T // 2) as mp:
                    for half in range(2):
                        m = mp * 2 + half
                        pe.wait_ge(hot_ready, c + 1)
                        pe.wait_ge(added, c * T + m + 1)
                        for t in range(CT):
                            for n, (a, w) in enumerate(NBLK):
                                mm = nc.tensor.matmul(ps[0:R, B * half + n, 0:w],
                                                      hot[b][0][:, t, bass.ds(m * R, R)],
                                                      hot[b][1][:, t, a:a + w],
                                                      start=(t == 0), stop=(t == CT - 1))
                        mm.then_inc(counted, 1)

            with pe.Fori(0, CHUNKS // 2) as cp:
                count_chunk(cp * 2, 0)
                count_chunk(cp * 2 + 1, 1)

            pe.wait_ge(consts, 4)
            pe.wait_ge(added, CHUNKS * T + 2)
            pe.wait_ge(bias_in, 16 * 7)
            fill(nc.tensor.transpose(bank("bias", 0)[:, 0:3 * K + G], bias_r[:, :], ident[0:3 * K + G, 0:3 * K + G]),
                 "bias", 0)
            pe.wait_ge(w_in, 16 * 5)
            for o in range(K):
                for i in range(K):
                    mm = nc.tensor.transpose(bank("fct", o)[:, i * P:(i + 1) * P], fcw[:, o, i * P:(i + 1) * P],
                                             ident[:, :])
                fill(mm, "fct", o)
            for n, (a, w) in enumerate(NBLK):
                wait_bank(pe, "deg", n)
                for s in range(T):
                    mm = nc.tensor.matmul(bank("deg", n)[:, 0:w], ones[0:R, :], adj[:, s, a:a + w],
                                          start=(s == 0), stop=(s == T - 1))
                fill(mm, "deg", n)

            def to_columns(stage):
                for t in range(T):
                    wait_bank(pe, stage, t)
                    for k in range(K):
                        mm = nc.tensor.transpose(bank(stage, t)[:, k * R:(k + 1) * R],
                                                 rows[:, t, k * P:(k + 1) * P], ident[0:R, 0:R])
                    fill(mm, stage, t)

            def to_rows(stage, cols, ready):
                for i in ready:
                    wait_emptied(pe, *i)
                for t in range(T):
                    wait_bank(pe, stage, t)
                    for k in range(K):
                        mm = nc.tensor.transpose(bank(stage, t)[0:R, k * P:(k + 1) * P],
                                                 cols[:, k, t * R:(t + 1) * R], ident[:, :])
                    fill(mm, stage, t)

            def dense(stage, pairs):
                for f in range(K):
                    for n, (a, w) in enumerate(NBLK):
                        wait_bank(pe, stage, f * B + n)
                        for j, (wt, cols) in enumerate(pairs):
                            for k in range(K):
                                mm = nc.tensor.matmul(bank(stage, f * B + n)[:, 0:w], wt[:, k, f * P:(f + 1) * P],
                                                      cols[:, k, a:a + w], start=(j + k == 0),
                                                      stop=(j == len(pairs) - 1 and k == K - 1))
                        fill(mm, stage, f * B + n)

            def gather(stage, before):
                for f in range(K):
                    for n, (a, w) in enumerate(NBLK):
                        wait_bank(pe, stage, f * B + n)
                        for s in range(T):
                            if f + n == 0:
                                wait_emptied(pe, before, s)
                            mm = nc.tensor.matmul(bank(stage, f * B + n)[:, 0:w], rows[:, s, f * P:(f + 1) * P],
                                                  adj[:, s, a:a + w], start=(s == 0), stop=(s == T - 1))
                        fill(mm, stage, f * B + n)

            pe.wait_ge(ln_rows, T)
            to_columns("xT")
            wait_bank(pe, "norm", 0)
            pe.wait_ge(norm_ready, 1)
            for t in range(T):
                mm = nc.tensor.transpose(bank("norm", 0)[0:R, t:t + 1], norm_b[0:1, t * R:(t + 1) * R],
                                         ident[0:1, 0:1])
            fill(mm, "norm", 0)
            for t in range(T):
                wait_emptied(pe, "xT", t)
            dense("h0", [(fct, colA)])
            to_rows("h0r", h0T, [("h0", i) for i in range(K * B)])
            gather("agg1", "h0r")
            pe.wait_ge(folded, 4 * (1 + K))
            for i in range(K * B):
                wait_emptied(pe, "agg1", i)
            dense("res1", [(w11, aggT), (w21, h0T)])
            to_rows("res1r", colA, [("res1", i) for i in range(K * B)])
            gather("agg2", "res1r")
            for i in range(K * B):
                wait_emptied(pe, "agg2", i)
            dense("res2", [(w12, aggT), (w22, h0T)])
            to_rows("res2r", colA, [("res2", i) for i in range(K * B)])
            pe.wait_ge(ln_rows, 2 * T)
            to_columns("x2T")
            pe.wait_ge(wx_in, 16 * 4)
            for t in range(T):
                wait_emptied(pe, "x2T", t)
            for g in range(G):
                for n, (a, w) in enumerate(NBLK):
                    wait_bank(pe, "z", g * B + n)
                    for k in range(K):
                        mm = nc.tensor.matmul(bank("z", g * B + n)[:, 0:w],
                                              wx[:, k, g // K, (g % K) * P:(g % K + 1) * P],
                                              colA[:, k, a:a + w], start=(k == 0), stop=(k == K - 1))
                    fill(mm, "z", g * B + n)

            def sweep(s, sw):
                for i in range(U if sw.parts else 0):
                    a, w = WINS[i // K]
                    j = i % K
                    if j == 0:
                        pe.wait_ge(oper_ready, s * U + (i + K - U))
                    pe.wait_ge(z_added, s * U + (i + 1 - U))
                    for q in range(4):
                        for n, part in enumerate(sw.parts):
                            for k in range(K):
                                mm = nc.tensor.matmul(ps[:, 4 * (j % 2) + q, 0:w],
                                                      w_part[part][:, k, q, j * P:(j + 1) * P],
                                                      oper[sw.source][:, k, a:a + w], start=(n + k == 0),
                                                      stop=(n == len(sw.parts) - 1 and k == K - 1))
                    mm.then_inc(unit_summed, 1)

            pe.wait_ge(low_ready, 4 * K)
            pe.wait_ge(started, 3)
            for i in range(G * B - BANKS, G * B):
                wait_emptied(pe, "z", i)
            all_sweeps(pe, sweep, {11: lambda: pe.wait_ge(started, 4)})
            pe.wait_ge(worst_ready, 1)
            nc.tensor.transpose(ps[0:1, 0, 0:P], worst[:, 0:1], ident[:, :]).then_inc(worst_turned, 1)
            pe.wait_ge(flag_ready, 1)
            with pe.If(pe.value_load(flag[0:1, 0:1], min_val=0, max_val=1) != 0):
                pe.wait_ge(wh_in, 16 * 4)
                with pe.Fori(0, N) as t:
                    pe.wait_ge(h_ready, t + 2)
                    for g in range(G):
                        for k in range(K):
                            mm = nc.tensor.matmul(ps[:, 0, g:g + 1], wh[:, k, g // K, (g % K) * P:(g % K + 1) * P],
                                                  h_now[:, k:k + 1], start=(k == 0), stop=(k == K - 1))
                    mm.then_inc(gates_ready, 1)
                pe.wait_ge(hT_ready, N)
            to_rows("out", hT, [])

        @block.scalar
        def _(act):
            def roots(n):
                act.wait_ge(var_ready, n)
                nc.scalar.activation(rstd[0:R, :], rstd[0:R, :], ACT.Sqrt).then_inc(std_ready, 1)

            def columns_out(stage, to, func, b):
                for f in range(K):
                    for n, (a, w) in enumerate(NBLK):
                        wait_filled(act, stage, f * B + n)
                        empty(nc.scalar.activation(to[:, f, a:a + w], bank(stage, f * B + n)[:, 0:w], func,
                                                   bias=bias[:, b + f:b + f + 1]), stage, f * B + n)

            roots(1)
            for n in range(B):
                wait_emptied(act, "deg", n)
            nc.scalar.activation(norm_b[:, :], norm_b[:, :], ACT.Sqrt).then_inc(root_ready, 1)
            wait_emptied(act, "bias", 0)
            columns_out("h0", h0T, ACT.Identity, 0)
            columns_out("res1", colA, ACT.Relu, K)
            columns_out("res2", colA, ACT.Relu, 2 * K)
            roots(2)
            for t in range(T):
                wait_filled(act, "x2T", t)
                empty(nc.scalar.copy(colA[:, :, t * R:(t + 1) * R],
                                     bank("x2T", t)[:, 0:K * R].rearrange("p (k r) -> p k r", k=K)), "x2T", t)
            m = 0
            for g in range(0, G, 2):
                for n, (a, w) in enumerate(NBLK):
                    wait_filled(act, "z", g * B + n)
                    empty(nc.scalar.activation(zT[:, g, a:a + w], bank("z", g * B + n)[:, 0:w], ACT.Identity,
                                               bias=bias[:, 3 * K + g:3 * K + g + 1]), "z", g * B + n)
                    if m < 4 * K:
                        act.wait_ge(piece_in[m % SLOTS], 16 * (m // SLOTS + 1))
                        nc.scalar.copy(w_part[0][:, m // 4, m % 4, :], split[m % SLOTS]).then_inc(high_ready, 1)
                    if 1 <= m <= 4 * K:
                        act.wait_ge(rest_ready, m)
                        nc.scalar.copy(w_part[1][:, (m - 1) // 4, (m - 1) % 4, :], split[(m - 1) % SLOTS])\
                            .then_inc(mid_ready, 1)
                    m += 1

            def sweep(s, sw):
                for i in range(U + 1):
                    if i < U:
                        a, w = WINS[i // K]
                        g = gate[i % LIVE][:, :, 0:w]
                        if sw.parts:
                            act.wait_ge(z_added, s * U + (i + 3 - U))
                        elif i >= LIVE:
                            act.wait_ge(oper_ready, i - LIVE + 1)
                        if sw.keep:
                            act.wait_ge(oper_ready, s * U + (i - LIVE + 1))
                        z = g if sw.parts and not sw.keep else z4[:, :, i % K, a:a + w]
                        nc.scalar.activation(g[:, 0:3, :], z[:, 0:3, :], ACT.Sigmoid).then_inc(unit_gated, 1)
                        nc.scalar.activation(g[:, 3, :], z[:, 3, :], ACT.Tanh).then_inc(unit_gated, 1)
                    if i >= 1:
                        w = WINS[(i - 1) // K][1]
                        act.wait_ge(cells_ready, s * U + i)
                        nc.scalar.activation(gate[(i - 1) % LIVE][:, 3, 0:w], cells[:, (i - 1) % K, 0:w],
                                             ACT.Tanh).then_inc(tanh_ready, 1)

            act.wait_ge(started, 3)
            for i in range(G * B - BANKS, G * B):
                wait_emptied(act, "z", i)
            all_sweeps(act, sweep)
            act.wait_ge(flag_ready, 1)
            with act.If(act.value_load(flag[0:1, 0:1], min_val=0, max_val=1) != 0):
                with act.Fori(0, N) as t:
                    act.wait_ge(z_ready, t + 1)
                    nc.scalar.activation(gates[:, 0:3 * K], z_now[:, 0:3 * K], ACT.Sigmoid).then_inc(act_ready, 1)
                    nc.scalar.activation(gates[:, 3 * K:G], z_now[:, 3 * K:G], ACT.Tanh).then_inc(act_ready, 1)
                    act.wait_ge(c_ready, t + 1)
                    nc.scalar.activation(tc[:, :], cell[:, :], ACT.Tanh).then_inc(tc_ready, 1)

        @block.vector
        def _(dve):
            link_n = [0]

            def link(ins):
                link_n[0] += 1
                ins.then_inc(chained, 1)
                dve.wait_ge(chained, link_n[0])

            def hot_rows(c, b):
                for s in range(2):
                    for t in range(CT):
                        ins = nc.vector.tensor_scalar(hot[b][s][:, t, :], iota,
                                                      edge_f[s][:, bass.ds(c * CT + t, 1)], None, ALU.is_equal)
                ins.then_inc(hot_ready, 1)

            def add_counts(c):
                with dve.Fori(0, T // 2) as mp:
                    for half in range(2):
                        m = mp * 2 + half
                        dve.wait_ge(counted, c * T + m + 1)
                        to = adj[:, bass.ds(m, 1), :].rearrange("p o n -> p (o n)")
                        got = ps[0:R, B * half:B * half + B, :].rearrange("p b n -> p (b n)")[:, 0:N]
                        nc.vector.tensor_tensor(to, to, got, ALU.add).then_inc(added, 1)

            def normalize(n):
                for t in range(T):
                    nc.vector.bn_stats(stats[0:R, t, :], xr[:, t, :]).then_inc(stat_ready, 1)
                dve.wait_ge(stat_ready, T * n)
                for t in range(T):
                    ins = nc.vector.bn_aggr(mv[0:R, t, :], stats[0:R, t, :])
                link(ins)
                nc.vector.tensor_scalar(rstd[0:R, :], mv[0:R, :, 1], EPS, None, ALU.add).then_inc(var_ready, 1)
                dve.wait_ge(std_ready, n)
                link(nc.vector.reciprocal(rstd[0:R, :], rstd[0:R, :]))
                for t in range(T):
                    nc.vector.tensor_scalar(rows[:, t, :], xr[:, t, :], mv[0:R, t, 0:1], rstd[0:R, t:t + 1],
                                            ALU.subtract, ALU.mult).then_inc(ln_rows, 1)

            def rows_out(stage):
                for t in range(T):
                    wait_filled(dve, stage, t)
                    empty(nc.vector.tensor_scalar(rows[:, t, :], bank(stage, t)[0:R, :], norm_c[0:R, t:t + 1],
                                                  None, ALU.mult), stage, t)

            def sums_out(stage):
                for f in range(K):
                    for n, (a, w) in enumerate(NBLK):
                        wait_filled(dve, stage, f * B + n)
                        empty(nc.vector.scalar_tensor_tensor(
                            out=aggT[:, f, a:a + w], in0=bank(stage, f * B + n)[:, 0:w], scalar=1.0 - ALPHA,
                            in1=norm_b[:, a:a + w], op0=ALU.mult, op1=ALU.mult), stage, f * B + n)

            dve.wait_ge(edges_in, 32)
            for s in range(2):
                nc.vector.tensor_copy(edge_f[s], edge_i[s]).then_inc(edges_f, 1)
            for s in range(2):
                nc.vector.memset(adj[:, s * T // 2:(s + 1) * T // 2, :], 0.0).then_inc(added, 1)
            dve.wait_ge(consts, 3)
            dve.wait_ge(edges_f, 2)
            hot_rows(0, 0)
            dve.wait_ge(x_in, 16)
            normalize(1)
            dve.wait_ge(added, 2)
            with dve.Fori(0, CHUNKS // 2 - 1) as cp:
                hot_rows(cp * 2 + 1, 1)
                add_counts(cp * 2)
                hot_rows(cp * 2 + 2, 0)
                add_counts(cp * 2 + 1)
            hot_rows(CHUNKS - 1, 1)
            add_counts(CHUNKS - 2)
            add_counts(CHUNKS - 1)

            wait_filled(dve, "bias", 0)
            empty(nc.vector.tensor_copy(bias[:, :], bank("bias", 0)[:, 0:3 * K + G]), "bias", 0)
            for o in range(K):
                wait_filled(dve, "fct", o)
                empty(nc.vector.tensor_copy(fct[:, :, o * P:(o + 1) * P],
                                            bank("fct", o).rearrange("p (k d) -> p k d", k=K)), "fct", o)
            for n, (a, w) in enumerate(NBLK):
                wait_filled(dve, "deg", n)
                empty(nc.vector.tensor_scalar(norm_b[:, a:a + w], bank("deg", n)[:, 0:w], 1.0, None, ALU.max),
                      "deg", n)
            dve.wait_ge(root_ready, 1)
            nc.vector.reciprocal(norm_b[:, :], norm_b[:, :]).then_inc(norm_ready, 1)
            for t in range(T):
                wait_filled(dve, "xT", t)
                empty(nc.vector.tensor_copy(colA[:, :, t * R:(t + 1) * R],
                                            bank("xT", t)[:, 0:K * R].rearrange("p (k r) -> p k r", k=K)), "xT", t)
            wait_filled(dve, "norm", 0)
            ins = nc.vector.tensor_copy(norm_c[0:R, :], bank("norm", 0)[0:R, 0:T])
            empty(ins, "norm", 0)
            wait_emptied(dve, "norm", 0)
            dve.wait_ge(w_in, 16 * 5)
            n = 0
            for layer, pair in ((1, (w11, w21)), (2, (w12, w22))):
                beta = math.log(LAMBDA / layer + 1.0)
                for w, c in zip(pair, (1.0, ALPHA)):
                    nc.vector.tensor_scalar(w, w, c * beta, None, ALU.mult).then_inc(folded, 1)
                    n += 1
                    dve.wait_ge(folded, n)
                    for k in range(K):
                        d = w[:, k, k * P:(k + 1) * P]
                        nc.vector.scalar_tensor_tensor(out=d, in0=ident[:, :], scalar=c * (1.0 - beta), in1=d,
                                                       op0=ALU.mult, op1=ALU.add).then_inc(folded, 1)
                        n += 1
            dve.wait_ge(norm_ready, 1)
            rows_out("h0r")
            sums_out("agg1")
            rows_out("res1r")
            sums_out("agg2")
            for t in range(T):
                wait_filled(dve, "res2r", t)
                empty(nc.vector.tensor_tensor(xr[:, t, :], xr[:, t, :], bank("res2r", t)[0:R, :], ALU.add),
                      "res2r", t)
            for t in range(T):
                wait_emptied(dve, "res2r", t)
            normalize(2)
            m = 0
            for g in range(1, G, 2):
                for n, (a, w) in enumerate(NBLK):
                    wait_filled(dve, "z", g * B + n)
                    empty(nc.vector.tensor_scalar(zT[:, g, a:a + w], bank("z", g * B + n)[:, 0:w],
                                                  bias[:, 3 * K + g:3 * K + g + 1], None, ALU.add),
                          "z", g * B + n)
                    if m < 4 * K:
                        dve.wait_ge(high_ready, m + 1)
                        nc.vector.tensor_tensor(split[m % SLOTS], split[m % SLOTS],
                                                w_part[0][:, m // 4, m % 4, :], ALU.subtract).then_inc(rest_ready, 1)
                    if 1 <= m <= 4 * K:
                        l = m - 1
                        dve.wait_ge(mid_ready, m)
                        nc.vector.tensor_tensor(w_part[2][:, l // 4, l % 4, :], split[l % SLOTS],
                                                w_part[1][:, l // 4, l % 4, :], ALU.subtract).then_inc(low_ready, 1)
                    m += 1
            for i in range(G * B - BANKS, G * B):
                wait_emptied(dve, "z", i)
            dve.wait_ge(low_ready, 4 * K)
            for o in range(3):
                nc.vector.memset(oper[o][:, :, 0:1], 0.0).then_inc(started, 1)
            for n in range(2):
                nc.vector.memset(change[:, n, :], 0.0).then_inc(z_added, 1)

            diffs = [0]

            def sweep(s, sw):
                for i in range(U + 2):
                    if i < U and sw.parts:
                        a, w = WINS[i // K]
                        half = 4 * (i % K % 2)
                        z = z4[:, :, i % K, a:a + w]
                        dve.wait_ge(oper_ready, s * U + (i - LIVE + 1))
                        dve.wait_ge(unit_summed, s * U + (i + 1 - U))
                        nc.vector.tensor_tensor(z if sw.keep else gate[i % LIVE][:, :, 0:w], z,
                                                ps[:, half:half + 4, 0:w], ALU.add).then_inc(z_added, 1)
                    if 1 <= i <= U:
                        l = i - 1
                        w, j = WINS[l // K][1], l % K
                        g = gate[l % LIVE][:, :, 0:w]
                        last = WINS[l // K - 1][1]
                        dve.wait_ge(ig_ready, s * U + (l + 1))
                        if l >= K:
                            dve.wait_ge(tanh_ready, s * U + (l - K + 1))
                            dve.wait_ge(cells_ready, s * U + (l - K + 1))
                        nc.vector.tensor_tensor_scan(cells[:, j, 0:w], g[:, 0, :], g[:, 1, :],
                                                     0.0 if l < K else cells[:, j, last - 1:last],
                                                     ALU.mult, ALU.add).then_inc(cells_ready, 1)
                    if i >= 2 and sw.taken:
                        l = i - 2
                        a, w = WINS[l // K]
                        j = l % K
                        g = gate[l % LIVE][:, 2, 0:w]
                        dve.wait_ge(hidden_ready, (s - 5) * U + (l + 1))
                        rest = hT[:, j, a:a + w] if sw.to is None else g
                        for n, o in enumerate(sw.taken):
                            if n:
                                dve.wait_ge(diff_step, diffs[0])
                            final = n == len(sw.taken) - 1
                            to = oper[sw.to][:, j, 1 + a:1 + a + w] if final and sw.to is not None else g
                            ins = nc.vector.tensor_tensor(to, rest, oper[o][:, j, 1 + a:1 + a + w], ALU.subtract)
                            rest = g
                            if final and sw.to is not None:
                                ins.then_inc(oper_ready, 1)
                            else:
                                diffs[0] += 1
                                ins.then_inc(diff_step, 1)
                            if sw.to is None and (n == 0 or final):
                                dve.wait_ge(diff_step, diffs[0])
                                ins = nc.vector.tensor_reduce(change[:, int(final), l:l + 1], g, AX.X, ALU.max,
                                                              apply_absolute_value=True)
                                ins.then_inc(oper_ready if final else diff_step, 1)
                                diffs[0] += int(not final)

            def zero_e():
                nc.vector.memset(oper[E_][:, :, 0:1], 0.0).then_inc(started, 1)

            all_sweeps(dve, sweep, {5: lambda: dve.wait_ge(zx_saved, 16), 11: zero_e})
            dve.wait_ge(oper_ready, 13 * U)
            for n in range(2):
                nc.vector.tensor_reduce(worst[:, n:n + 1], change[:, n, :], AX.X, ALU.max).then_inc(diff_step, 1)
            diffs[0] += 2
            dve.wait_ge(diff_step, diffs[0])
            nc.vector.tensor_scalar(worst[:, :], worst[:, :], 1.0 / CHANGE_LIMIT, None, ALU.mult).then_inc(diff_step, 1)
            diffs[0] += 1
            dve.wait_ge(diff_step, diffs[0])
            nc.vector.scalar_tensor_tensor(out=worst[:, 0:1], in0=worst[:, 0:1], scalar=CHANGE_LIMIT / REST_LIMIT,
                                           in1=worst[:, 1:2], op0=ALU.mult, op1=ALU.max).then_inc(worst_ready, 1)
            dve.wait_ge(worst_turned, 1)
            nc.vector.tensor_reduce(far[:, :], ps[0:1, 0, 0:P], AX.X, ALU.max).then_inc(diff_step, 1)
            diffs[0] += 1
            dve.wait_ge(diff_step, diffs[0])
            nc.vector.tensor_scalar(flag[:, :], far[:, :], 1.0, None, ALU.is_gt).then_inc(flag_ready, 1)
            dve.wait_ge(flag_ready, 1)
            with dve.If(dve.value_load(flag[0:1, 0:1], min_val=0, max_val=1) != 0):
                dve.wait_ge(zx_back, 16)
                nc.vector.memset(cell[:, :], 0.0).then_inc(h_ready, 1)
                nc.vector.memset(h_now[:, :], 0.0).then_inc(h_ready, 1)
                dve.wait_ge(h_ready, 2)
                with dve.Fori(0, N) as t:
                    dve.wait_ge(gates_ready, t + 1)
                    z_t = zT[:, :, bass.ds(t, 1)].rearrange("p g o -> p (g o)")
                    nc.vector.tensor_tensor(z_now[:, :], z_t, ps[:, 0, 0:G], ALU.add).then_inc(z_ready, 1)
                    dve.wait_ge(act_ready, t * 2 + 2)
                    nc.vector.tensor_tensor(ig[:, :], gates[:, K:2 * K], gates[:, 3 * K:G], ALU.mult).then_inc(cell_step, 1)
                    nc.vector.tensor_tensor(fc[:, :], gates[:, 0:K], cell[:, :], ALU.mult).then_inc(cell_step, 1)
                    dve.wait_ge(cell_step, t * 2 + 2)
                    nc.vector.tensor_tensor(cell[:, :], ig[:, :], fc[:, :], ALU.add).then_inc(c_ready, 1)
                    dve.wait_ge(tc_ready, t + 1)
                    dve.wait_ge(c_ready, t + 1)
                    nc.vector.tensor_tensor(h_now[:, :], gates[:, 2 * K:3 * K], tc[:, :], ALU.mult).then_inc(h_ready, 1)
                    h_t = hT[:, :, bass.ds(t, 1)].rearrange("p k o -> p (k o)")
                    nc.vector.tensor_tensor(h_t, gates[:, 2 * K:3 * K], tc[:, :], ALU.mult).then_inc(hT_ready, 1)
            for t in range(T):
                wait_filled(dve, "out", t)
                empty(nc.vector.tensor_tensor(xr[:, t, :], xr[:, t, :], bank("out", t)[0:R, :], ALU.add), "out", t)


_INS = ["x", "src", "dst", "L0_gnn_fc_w", "L0_gnn_fc_b", "L0_gnn_w1_1", "L0_gnn_w2_1", "L0_gnn_b_1",
        "L0_gnn_w1_2", "L0_gnn_w2_2", "L0_gnn_b_2", "L0_ffn_W_f", "L0_ffn_b_f", "L0_ffn_W_i", "L0_ffn_b_i",
        "L0_ffn_W_c", "L0_ffn_b_c", "L0_ffn_W_o", "L0_ffn_b_o"]


def kernel(**inputs):
    import numpy as np
    import concourse.bacc as bacc
    from concourse import mybir as mb
    from concourse.bass_utils import run_bass_kernel_spmd

    nc = bacc.Bacc("TRN2", target_bir_lowering=False, num_devices=1)
    arrays, args = {}, []
    for name in _INS:
        a = np.ascontiguousarray(inputs[name])
        arrays[f"in_{name}"] = a
        args.append(nc.dram_tensor(f"in_{name}", a.shape, mb.dt.from_np(a.dtype), kind="ExternalInput").ap())
    out = nc.dram_tensor("out_0", inputs["x"].shape, mb.dt.float32, kind="ExternalOutput").ap()
    gnn_lstm_kernel(nc, *args, out)
    return run_bass_kernel_spmd(nc, [arrays], core_ids=[0]).results[0]["out_0"]
```

```python
from contextlib import ExitStack
import math

import concourse.bass as bass
from concourse import mybir

F32 = mybir.dt.float32
BF16 = mybir.dt.bfloat16
I32 = mybir.dt.int32
I16 = mybir.dt.int16
ALU = mybir.AluOpType
ACT = mybir.ActivationFunctionType
AX = mybir.AxisListType

P = 128
BANKS = 8
BANK = 512
ALPHA = 0.1
LAMBDA = 1.0
EPS = 1e-5


def gnn_lstm_kernel(nc, x, src, dst, fc_w, fc_b, w1_1, w2_1, b_1, w1_2, w2_2, b_2,
                    W_f, b_f, W_i, b_i, W_c, b_c, W_o, b_o, out):
    N, D = x.shape
    E = src.shape[0]
    K = D // P
    R = 125
    T = N // R
    EP = E // (2 * R)
    G = 4 * K
    NBLK = [(a, min(BANK, N - a)) for a in range(0, N, BANK)]
    B = len(NBLK)
    PER = BANK // R
    CB = -(-T // PER)
    DEG_AT = (T - PER * (CB - 1)) * R
    HOT = T * R + P - R + 3
    assert T * R == N and EP * 2 * R == E and T % 2 == 0 and EP <= P and 2 * CB < BANKS

    with ExitStack() as ctx:
        def sb(name, shape, dt=F32):
            return ctx.enter_context(nc.sbuf_tensor(name, shape, dt))

        def sem(name):
            return ctx.enter_context(nc.semaphore(name))

        X_AT = 0
        ROWS_AT = X_AT + T * D
        LEFT_AT = ROWS_AT + 3 * T * D // 2
        GNN_W_AT = LEFT_AT + 2 * D
        A_AT = GNN_W_AT + 4 * K * D
        SPLIT_AT = ROWS_AT + G * N
        WX_AT = SPLIT_AT + 3 * D
        COL_AT = max(A_AT + T * N, WX_AT + G * D)
        NORM_AT = COL_AT + 3 * K * N
        FCW_AT = NORM_AT - K * D
        FCT_AT = FCW_AT - K * D
        XT_AT = WX_AT + G * D
        W_AT = XT_AT + K * N
        HALF = K * G * P // 2
        W_END = W_AT + 3 * HALF
        END = max(W_END, NORM_AT + N)
        arena = sb("arena", [P, END])

        def region(at, n, parts=P):
            return arena[0:parts, at:at + n]

        xr = region(X_AT, T * D, R).rearrange("p (t d) -> p t d", t=T)
        rows = region(ROWS_AT, T * D, R).rearrange("p (t d) -> p t d", t=T)
        fcw, fct = [region(a, K * D).rearrange("p (k d) -> p k d", k=K) for a in (FCW_AT, FCT_AT)]
        w11, w21, w12, w22 = [region(GNN_W_AT + n * K * D, K * D).rearrange("p (k d) -> p k d", k=K)
                              for n in range(4)]
        adj = [region(A_AT + n * T * N // 2, T * N // 2, R).bitcast(BF16).rearrange("p (t n) -> p t n", t=T)
               for n in range(2)]
        row_part = [region(ROWS_AT + n * T * D // 2, T * D // 2, R).bitcast(BF16)
                    .rearrange("p (t d) -> p t d", t=T) for n in range(3)]
        left = [region(LEFT_AT + n * D, D, R) for n in range(2)]
        colA, h0T, aggT = [region(COL_AT + n * K * N, K * N).rearrange("p (k n) -> p k n", k=K)
                           for n in range(3)]
        at = [COL_AT]

        def early(n, parts):
            at[0] += n
            assert at[0] <= FCT_AT
            return region(at[0] - n, n, parts)

        edge_i = [early(2 * R, EP).bitcast(I32) for s in range(2)]
        edge_f = [early(2 * R, EP) for s in range(2)]
        edge_c = early(4 * EP, R).rearrange("p (s h e) -> p s h e", s=2, h=2)
        iota = early(HOT // 2, R).bitcast(I16)
        hot_src = [early(HOT // 2, R).bitcast(BF16) for h in range(4)]
        hot_dst = [early((R + 1) // 2, R).bitcast(BF16)[:, 0:R] for h in range(4)]
        block_counts = [early(N, R) for h in range(2)]
        zeros = early(BANK // 2, R).bitcast(BF16)
        ones = early(P // 2, R).bitcast(BF16)
        block_at = early(T, EP)
        pair_up = early(1, EP)
        pair_down = early(1, EP)
        reach = early(2, EP)
        meets = early(2 * T, EP).rearrange("p (s t) -> p s t", s=2)
        keys = early(2 * T, EP).rearrange("p (s t) -> p s t", s=2)
        ends = early(2 * T, EP).rearrange("p (s t) -> p s t", s=2)
        span = early(3 * T, 1).rearrange("p (s t) -> p s t", s=3)
        span_up = early(T, 1)
        halves = early(T, 1).bitcast(I32)
        spans = early(3 * T, 1).bitcast(I32).rearrange("p (s t) -> p s t", s=3)
        zT = region(ROWS_AT, G * N).rearrange("p (g n) -> p g n", g=G)
        wx = region(WX_AT, G * D).rearrange("p (k g d) -> p k g d", k=K, g=4)
        xT = region(XT_AT, K * N).rearrange("p (k n) -> p k n", k=K)
        w_part = [region(W_AT + n * HALF, HALF).bitcast(BF16).rearrange("p (k g d) -> p k g d", k=K, g=4)
                  for n in range(3)]
        SLOTS = 3
        split = [region(SPLIT_AT + n * D, D) for n in range(SLOTS)]
        WIN = 418
        WINS = [(a, min(WIN, N - a) if a == 0 else 416) for a in (0, 418, 834)]
        assert sum(w for _, w in WINS) == N
        Q = len(WINS)
        U = Q * K
        OPN = K * (N + 2) // 2
        LIVE = 3
        gates_at = SPLIT_AT + 3 * OPN
        cells_at = gates_at + LIVE * 4 * WIN
        assert cells_at + K * WIN <= W_AT
        spots = [SPLIT_AT, SPLIT_AT + OPN, SPLIT_AT + 2 * OPN, W_END - OPN]
        oper = [region(o, OPN).bitcast(BF16).rearrange("p (k n) -> p k n", k=K) for o in spots]
        gate = [region(gates_at + n * 4 * WIN, 4 * WIN).rearrange("p (g n) -> p g n", g=4) for n in range(LIVE)]
        without_a = [region(spots[1] + n * WIN, WIN) for n in range(LIVE)]
        rest = [region(at_, WIN) for at_ in (spots[1] + 3 * WIN, spots[1] + 4 * WIN, cells_at + K * WIN)]
        assert 5 * WIN <= OPN and cells_at + (K + 1) * WIN <= W_AT and len(rest) == LIVE
        state = [region(W_AT + 2 * HALF + n * WIN, WIN) for n in range(LIVE)]
        assert W_AT + 2 * HALF + LIVE * WIN <= W_END - OPN
        cells = region(cells_at, K * WIN).rearrange("p (k n) -> p k n", k=K)
        hT = region(W_AT + HALF, K * N).rearrange("p (k n) -> p k n", k=K)
        assert W_AT + HALF + K * N <= W_END - OPN
        z4 = zT.rearrange("p (g k) n -> p g k n", g=4)
        wh = region(SPLIT_AT, G * D).rearrange("p (k g d) -> p k g d", k=K, g=4)
        norm_b = region(NORM_AT, N)
        out_rows = region(ROWS_AT, T * D, R).rearrange("p (t d) -> p t d", t=T)
        zx_kept = nc.dram_tensor("zx_kept", [P, G * N], F32).ap()

        ident = sb("ident", [P, P])
        ones_f = sb("ones_f", [1, T])
        sums = sb("sums", [P, 2, T])
        minus_mean = sb("minus_mean", [P, T])
        most_of = sb("most_of", [P, 1])
        most = sb("most", [1, 1])
        many_flag = sb("many_flag", [1, 1], I32)
        norm_c = sb("norm_c", [P, T])
        bias_r = sb("bias_r", [3 * K + G, P])
        bias = sb("bias", [P, 3 * K + G])
        stats = sb("stats", [P, T, 6])
        mv = sb("mv", [P, T, 2])
        rstd = sb("rstd", [P, T])
        cell = sb("cell", [P, K])
        h_now = sb("h_now", [P, K])
        z_now = sb("z_now", [P, G])
        gates = sb("gates", [P, G])
        ig = sb("ig", [P, K])
        fc = sb("fc", [P, K])
        tc = sb("tc", [P, K])
        change = sb("change", [P, 2, U])
        worst = sb("worst", [P, 2])
        far = sb("far", [1, 1])
        flag = sb("flag", [1, 1], I32)
        ps = ctx.enter_context(nc.psum_tensor("ps", [P, BANKS, BANK], F32))

        edges_in = sem("edges_in")
        x_in = sem("x_in")
        w_in = sem("w_in")
        bias_in = sem("bias_in")
        wx_in = sem("wx_in")
        wh_in = sem("wh_in")
        stored = sem("stored")
        consts = sem("consts")
        edges_f = sem("edges_f")
        edges_turned = sem("edges_turned")
        edges_ready = sem("edges_ready")
        keys_ready = sem("keys_ready")
        ends_ready = sem("ends_ready")
        spans_ready = sem("spans_ready")
        zeros_ready = sem("zeros_ready")
        hot_ready = sem("hot_ready")
        sums_ready = sem("sums_ready")
        means_ready = sem("means_ready")
        squares_ready = sem("squares_ready")
        scale_ready = sem("scale_ready")
        degrees_ready = sem("degrees_ready")
        most_ready = sem("most_ready")
        many_ready = sem("many_ready")
        counts_split = sem("counts_split")
        part1_ready = sem("part1_ready")
        part2_ready = sem("part2_ready")
        part3_ready = sem("part3_ready")
        hot_used = sem("hot_used")
        counted = sem("counted")
        block_out = sem("block_out")
        filled = [sem(f"filled{b}") for b in range(BANKS)]
        emptied = [sem(f"emptied{b}") for b in range(BANKS)]
        chained = sem("chained")
        stat_ready = sem("stat_ready")
        var_ready = sem("var_ready")
        std_ready = sem("std_ready")
        root_ready = sem("root_ready")
        norm_ready = sem("norm_ready")
        cell_step = sem("cell_step")
        hT_ready = sem("hT_ready")
        folded = sem("folded")
        h_ready = sem("h_ready")
        gates_ready = sem("gates_ready")
        z_ready = sem("z_ready")
        act_ready = sem("act_ready")
        c_ready = sem("c_ready")
        tc_ready = sem("tc_ready")
        ln_rows = sem("ln_rows")
        state_out = sem("state_out")
        rest_taken = sem("rest_taken")
        piece_in = [sem(f"piece_in{n}") for n in range(SLOTS)]
        high_ready = sem("high_ready")
        rest_ready = sem("rest_ready")
        mid_ready = sem("mid_ready")
        low_ready = sem("low_ready")
        zx_saved = sem("zx_saved")
        zx_back = sem("zx_back")
        started = sem("started")
        unit_summed = sem("unit_summed")
        z_added = sem("z_added")
        unit_gated = sem("unit_gated")
        ig_ready = sem("ig_ready")
        cells_ready = sem("cells_ready")
        tanh_ready = sem("tanh_ready")
        hidden_ready = sem("hidden_ready")
        oper_ready = sem("oper_ready")
        diff_step = sem("diff_step")
        worst_ready = sem("worst_ready")
        worst_turned = sem("worst_turned")
        flag_ready = sem("flag_ready")

        group_ends = [0, NBLK[0][1] // R, (NBLK[1][0] + NBLK[1][1]) // R, T]
        GROUPS = [range(a, b) for a, b in zip(group_ends, group_ends[1:])]

        def turned(stage, rows_):
            columns = [0, K * (B - 1), K * (B - 1) + K // 2, K * B]
            return [product for n in range(3) for product in
                    [(stage, i) for i in range(columns[n], columns[n + 1])] + [(rows_, t) for t in GROUPS[n]]]

        def all_of(stage, n):
            return [(stage, i) for i in range(n)]

        NORM_AFTER = K
        X_LATE = 2
        order = (all_of("bias", 1) + all_of("fct", K) + all_of("xT", T)
                 + turned("h0", "h0r")[:NORM_AFTER] + all_of("norm", 1) + turned("h0", "h0r")[NORM_AFTER:]
                 + all_of("most", 1) + all_of("agg1", K * B) + turned("res1", "res1r")
                 + all_of("agg2", K * B) + turned("res2", "res2r")
                 + [("x2T", t) for g in GROUPS[:2] for t in g] + all_of("z", X_LATE)
                 + [("x2T", t) for t in GROUPS[2]] + all_of("z", G * B)[X_LATE:] + all_of("out", T)
                 + all_of("again", T))
        number = {product: n for n, product in enumerate(order)}
        assert len(number) == len(order)

        def bank(stage, i):
            return ps[:, number[stage, i] % BANKS, :]

        def wait_filled(eng, stage, i):
            n = number[stage, i]
            eng.wait_ge(filled[n % BANKS], n // BANKS + 1)

        def wait_emptied(eng, stage, i):
            n = number[stage, i]
            eng.wait_ge(emptied[n % BANKS], n // BANKS + 1)

        def wait_first(eng, stage, n):
            for i in range(n):
                if all(number[stage, j] % BANKS != number[stage, i] % BANKS for j in range(i + 1, n)):
                    wait_emptied(eng, stage, i)

        def wait_bank(eng, stage, i):
            n = number[stage, i]
            if n >= BANKS:
                eng.wait_ge(emptied[n % BANKS], n // BANKS)

        def fill(ins, stage, i):
            ins.then_inc(filled[number[stage, i] % BANKS], 1)

        def empty(ins, stage, i):
            ins.then_inc(emptied[number[stage, i] % BANKS], 1)

        REST_LIMIT = 2.0 ** -5
        CHANGE_LIMIT = 2.0 ** -15

        class Sweep:
            def __init__(self, source, parts, keep, taken, to):
                self.source = source
                self.parts = parts
                self.keep = keep
                self.taken = taken
                self.to = to
                self.third_free = bool(taken) and len(parts) < 3

        A, D_, E_ = 0, 2, 3

        def all_sweeps(eng, unit, steps, before=None):
            lag = max(steps)
            before = before or {}

            def run(s, sw, last):
                for i in range(U):
                    for k in steps:
                        if i >= k:
                            unit(s, sw, i - k, k)
                        elif last:
                            unit(s - 1, last, i - k + U, k)
                return sw

            first_ = run(0, Sweep(None, (), False, (), 0), None)
            with eng.Fori(0, 2) as r:
                odd = run(r * 2 + 1, Sweep(0, (0,), False, (), 1), first_)
                last = run(r * 2 + 2, Sweep(1, (0,), False, (), 0), odd)
            for s, sw in ((5, Sweep(A, (0, 1, 2), True, (A,), 1)),
                          (6, Sweep(1, (0,), False, (A,), 2)),
                          (7, Sweep(2, (0,), False, (A,), 1)),
                          (8, Sweep(1, (0,), False, (A,), D_)),
                          (9, Sweep(D_, (0, 1), True, (A, D_), 1)),
                          (10, Sweep(1, (0,), False, (A, D_), E_)),
                          (11, Sweep(E_, (0,), False, (A, D_, E_), None))):
                if s in before:
                    before[s]()
                last = run(s, sw, last)
            for i in range(U, U + lag):
                for k in steps:
                    if k > i - U:
                        unit(11, last, i - k, k)

        block = ctx.enter_context(nc.Block())

        @block.sync
        def _(sp):
            for s, e in ((0, src), (1, dst)):
                sp.dma_start(edge_i[s], e.rearrange("(p t) -> p t", p=EP)).then_inc(edges_in, 16)
            sp.dma_start(xr, x.rearrange("(t p) d -> p t d", p=R)).then_inc(x_in, 16)
            at = 0
            for b in (fc_b, b_1, b_2, b_f, b_i, b_o, b_c):
                sp.dma_start(bias_r[at:at + K, :], b.rearrange("(k p) -> k p", p=P)).then_inc(bias_in, 16)
                at += K
            for to, w in ((fcw, fc_w), (w11, w1_1), (w21, w2_1), (w12, w1_2), (w22, w2_2)):
                sp.dma_start(to, w.rearrange("(k p) d -> p k d", p=P)).then_inc(w_in, 16)
            wait_first(sp, "agg2", K * B)
            for g, w in enumerate((W_f, W_i, W_o, W_c)):
                sp.dma_start(wx[:, :, g, :], w[0:D, :].rearrange("(k p) d -> p k d", p=P)).then_inc(wx_in, 16)
            wait_first(sp, "res2", K * B)
            for n in range(K * 4):
                k, g = n // 4, n % 4
                if n >= SLOTS:
                    sp.wait_ge(low_ready, n - SLOTS + 1)
                sp.dma_start(split[n % SLOTS], (W_f, W_i, W_o, W_c)[g][D + k * P:D + (k + 1) * P, :])\
                    .then_inc(piece_in[n % SLOTS], 16)
            wait_first(sp, "z", G * B)
            sp.dma_start(zx_kept, region(ROWS_AT, G * N)).then_inc(zx_saved, 16)
            sp.wait_ge(zx_saved, 16)
            out_v = out.rearrange("(t p) d -> p t d", p=R)
            for t in range(T):
                wait_emptied(sp, "out", t)
                sp.dma_start(out_v[:, t, :], out_rows[:, t, :]).then_inc(stored, 16)
            sp.wait_ge(stored, 16 * T)
            sp.wait_ge(flag_ready, 1)
            with sp.If(sp.value_load(flag[0:1, 0:1], min_val=0, max_val=1) != 0):
                sp.dma_start(region(ROWS_AT, G * N), zx_kept).then_inc(zx_back, 16)
                for g, w in enumerate((W_f, W_i, W_o, W_c)):
                    sp.dma_start(wh[:, :, g, :], w[D:2 * D, :].rearrange("(k p) d -> p k d", p=P)).then_inc(wh_in, 16)
                for t in range(T):
                    wait_emptied(sp, "again", t)
                    sp.dma_start(out_v[:, t, :], xr[:, t, :]).then_inc(stored, 16)
                sp.wait_ge(stored, 32 * T)

        @block.gpsimd
        def _(pool):
            nc.gpsimd.memset(ident[:, :], 0.0).then_inc(consts, 1)
            nc.gpsimd.iota(iota, [[1, HOT]], base=0, channel_multiplier=0).then_inc(consts, 1)
            for to, pattern, base, step in ((block_at, [[R, T]], 0, 0), (pair_up, [[0, 1]], 1, 1),
                                            (pair_down, [[0, 1]], EP, -1)):
                nc.gpsimd.iota(to, pattern, base=base, channel_multiplier=step,
                               allow_small_or_imprecise_dtypes=True).then_inc(consts, 1)
            nc.gpsimd.memset(ones_f[:, :], 1.0).then_inc(consts, 1)
            nc.gpsimd.memset(ones, 1.0).then_inc(consts, 1)
            pool.wait_ge(consts, 7)
            nc.gpsimd.affine_select(out=ident[:, :], in_=ident[:, :], compare_op=ALU.not_equal, fill=1.0,
                                    base=0, pattern=[[-1, P]], channel_multiplier=1).then_inc(consts, 1)
            pool.wait_ge(keys_ready, 2)
            nc.gpsimd.partition_all_reduce(ends[:, :, :], keys[:, :, :], EP, bass.bass_isa.ReduceOp.max)\
                .then_inc(ends_ready, 1)
            pool.wait_ge(sums_ready, T)
            nc.gpsimd.tensor_scalar(minus_mean[0:R, :], sums[0:R, 0, :], -1.0 / D, 0.0, ALU.mult, ALU.add)\
                .then_inc(means_ready, 1)
            pool.wait_ge(squares_ready, T)
            nc.gpsimd.tensor_scalar(rstd[0:R, :], sums[0:R, 1, :], 1.0 / D, EPS, ALU.mult, ALU.add)\
                .then_inc(var_ready, 1)
            for half in range(2):
                nc.gpsimd.memset(block_counts[half], 0.0).then_inc(counts_split, 1)
            with pool.Fori(0, T // 2) as np_:
                for half in range(2):
                    n = np_ * 2 + half
                    pool.wait_ge(block_out, n + 3)
                    block_ = block_counts[half].rearrange("p (m d) -> p m d", m=T)
                    high, low = [a[:, :, bass.ds(n * R, R)] for a in adj]
                    nc.gpsimd.tensor_tensor(low, block_, high, ALU.subtract).then_inc(counts_split, 1)
            for n in range(2 * T):
                pool.wait_ge(part2_ready, n + 1)
                nc.gpsimd.tensor_tensor(row_part[2][:, n % T, :], left[n % 2], row_part[1][:, n % T, :],
                                        ALU.subtract).then_inc(part3_ready, 1)

            def unit(s, sw, i, k):
                a, w = WINS[i // K]
                j = i % K
                g = gate[i % LIVE][:, :, 0:w]
                if k == 0:
                    pool.wait_ge(unit_gated, s * (2 * U) + (2 * i + 2))
                    nc.gpsimd.tensor_tensor(g[:, 1, :], g[:, 1, :], g[:, 3, :], ALU.mult).then_inc(ig_ready, 1)
                    return
                h = hT[:, j, a:a + w] if sw.to is None else state[i % LIVE][:, 0:w]
                if k == 2:
                    if len(sw.taken) > 1:
                        h_a = h
                        if sw.to is None:
                            h_a = without_a[i % LIVE][:, 0:w]
                            if i >= LIVE:
                                pool.wait_ge(oper_ready, s * U + (i - LIVE + 1))
                        pool.wait_ge(state_out, (s - 6) * U + (i + 1))
                        nc.gpsimd.tensor_tensor(h_a, h, oper[A][:, j, 1 + a:1 + a + w], ALU.subtract)\
                            .then_inc(hidden_ready, 1)
                    return
                pool.wait_ge(tanh_ready, s * U + (i + 1))
                if sw.third_free:
                    if sw.to is not None or i < LIVE:
                        pool.wait_ge(oper_ready, s * U + (i - LIVE + 1))
                    nc.gpsimd.tensor_tensor(h, g[:, 2, :], g[:, 3, :], ALU.mult).then_inc(state_out, 1)
                    return
                if sw.taken:
                    h, done = g[:, 2, :], hidden_ready
                else:
                    h, done = oper[sw.to][:, j, 1 + a:1 + a + w], oper_ready
                nc.gpsimd.tensor_tensor(h, g[:, 2, :], g[:, 3, :], ALU.mult).then_inc(done, 1)

            pool.wait_ge(started, 3)
            all_sweeps(pool, unit, (0, 2, 1))

        @block.tensor
        def _(pe):
            pe.wait_ge(consts, 8)
            pe.wait_ge(edges_f, 2)
            for s in range(2):
                for h in range(2):
                    mm = nc.tensor.transpose(ps[0:R, BANKS - 1, (2 * s + h) * EP:(2 * s + h + 1) * EP],
                                             edge_f[s][:, h * R:(h + 1) * R], ident[0:EP, 0:EP])
            mm.then_inc(edges_turned, 1)

            pe.wait_ge(zeros_ready, 1)
            pe.wait_ge(spans_ready, 1)
            with pe.Fori(0, T // 2) as np_:
                for half in range(2):
                    n = np_ * 2 + half
                    count = pe.value_load(spans[0:1, 1, bass.ds(n, 1)], min_val=1, max_val=EP // 2)
                    base = pe.value_load(spans[0:1, 2, bass.ds(n, 1)], min_val=0, max_val=T * EP)
                    pe.wait_ge(block_out, n + 1)
                    for b in range(CB):
                        nc.tensor.matmul(ps[:, CB * half + b, 0:DEG_AT + R if b == CB - 1 else PER * R],
                                         zeros[:, 0:P], zeros[:, 0:DEG_AT + R if b == CB - 1 else PER * R],
                                         start=True, stop=False, skip_group_check=True)
                    nc.tensor.nop()
                    with pe.Fori(0, count) as i:
                        for k in range(4):
                            pe.wait_ge(hot_ready, (base + i) * 4 + (k + 1))
                            nc.tensor.matmul(ps[:, CB * half + CB - 1, DEG_AT:DEG_AT + R], ones, hot_dst[k],
                                             start=False, stop=False, skip_group_check=True)
                            for m in range(T):
                                mm = nc.tensor.matmul(ps[:, CB * half + m // PER, m % PER * R:(m % PER + 1) * R],
                                                      hot_src[k][:, m * R:m * R + P], hot_dst[k],
                                                      start=False, stop=False, skip_group_check=True)
                            mm.then_inc(hot_used, 1)
                    nc.tensor.matmul(ps[:, CB * half, 0:1], zeros[:, 0:P], zeros[:, 0:1],
                                     start=False, stop=True, skip_group_check=True).then_inc(counted, 1)

            pe.wait_ge(block_out, T + 2)
            pe.wait_ge(bias_in, 16 * 7)
            fill(nc.tensor.transpose(bank("bias", 0)[:, 0:3 * K + G], bias_r[:, :], ident[0:3 * K + G, 0:3 * K + G]),
                 "bias", 0)
            pe.wait_ge(w_in, 16 * 5)
            for o in range(K):
                for i in range(K):
                    mm = nc.tensor.transpose(bank("fct", o)[:, i * P:(i + 1) * P], fcw[:, o, i * P:(i + 1) * P],
                                             ident[:, :])
                fill(mm, "fct", o)
            def tile_to_columns(stage, t):
                wait_bank(pe, stage, t)
                for k in range(K):
                    mm = nc.tensor.transpose(bank(stage, t)[:, k * R:(k + 1) * R],
                                             rows[:, t, k * P:(k + 1) * P], ident[0:R, 0:R])
                fill(mm, stage, t)

            def tile_to_rows(stage, t, cols):
                wait_bank(pe, stage, t)
                for k in range(K):
                    mm = nc.tensor.transpose(bank(stage, t)[0:R, k * P:(k + 1) * P],
                                             cols[:, k, t * R:(t + 1) * R], ident[:, :])
                fill(mm, stage, t)

            def dense(stage, rows_, pairs, out_cols, sources):
                for st, i in turned(stage, rows_):
                    if st == rows_:
                        for m in range(((i + 1) * R - 1) // BANK + 1):
                            for f in range(K):
                                wait_emptied(pe, stage, m * K + f)
                        tile_to_rows(rows_, i, out_cols)
                        continue
                    if stage == "h0" and i == NORM_AFTER:
                        norm_to_rows()
                    n, f = i // K, i % K
                    a, w = NBLK[n]
                    wait_bank(pe, stage, i)
                    for j, (wt, cols) in enumerate(pairs):
                        if f == 0:
                            for source in sources[j](n):
                                wait_emptied(pe, *source)
                        for k in range(K):
                            mm = nc.tensor.matmul(bank(stage, i)[:, 0:w], wt[:, k, f * P:(f + 1) * P],
                                                  cols[:, k, a:a + w], start=(j + k == 0),
                                                  stop=(j == len(pairs) - 1 and k == K - 1))
                    fill(mm, stage, i)

            def gather(stage, n_before):
                with pe.If(pe.value_load(many_flag[0:1, 0:1], min_val=0, max_val=1) != 0):
                    pe.wait_ge(part3_ready, n_before + T)
                    for i in range(K * B):
                        f, (a, w) = i // B, NBLK[i % B]
                        wait_bank(pe, stage, i)
                        for s in range(T):
                            for m in range(6):
                                mm = nc.tensor.matmul(bank(stage, i)[:, 0:w],
                                                      row_part[m // 2][:, s, f * P:(f + 1) * P],
                                                      adj[m % 2][:, s, a:a + w], start=(s == 0 and m == 0),
                                                      stop=(s == T - 1 and m == 5))
                        fill(mm, stage, i)
                with pe.Else():
                    for f in range(K):
                        for n in range(B):
                            wait_bank(pe, stage, f * B + n)
                        for s in range(T):
                            pe.wait_ge(part3_ready, n_before + s + 1)
                            for m in range(3):
                                for n, (a, w) in enumerate(NBLK):
                                    mm = nc.tensor.matmul(bank(stage, f * B + n)[:, 0:w],
                                                          row_part[m][:, s, f * P:(f + 1) * P],
                                                          adj[0][:, s, a:a + w], start=(s == 0 and m == 0),
                                                          stop=(s == T - 1 and m == 2))
                                    if s == T - 1 and m == 2:
                                        fill(mm, stage, f * B + n)

            for t in range(T):
                pe.wait_ge(ln_rows, t + 1)
                tile_to_columns("xT", t)
            def norm_to_rows():
                wait_bank(pe, "norm", 0)
                pe.wait_ge(norm_ready, 1)
                for t in range(T):
                    mm = nc.tensor.transpose(bank("norm", 0)[0:R, t:t + 1], norm_b[0:1, t * R:(t + 1) * R],
                                             ident[0:1, 0:1])
                fill(mm, "norm", 0)

            def x_tiles(n):
                a, w = NBLK[n]
                return [("xT", t) for t in range((a + w - 1) // R + 1)]

            def h0_before(n):
                return []

            def agg_block(stage):
                return lambda n: [(stage, f * B + n) for f in range(K)]

            dense("h0", "h0r", [(fct, colA)], h0T, [x_tiles])
            pe.wait_ge(most_ready, 1)
            wait_bank(pe, "most", 0)
            fill(nc.tensor.transpose(bank("most", 0)[0:1, 0:R], most_of[0:R, :], ident[0:R, 0:R]), "most", 0)
            pe.wait_ge(many_ready, 1)
            pe.wait_ge(counts_split, T + 2)
            gather("agg1", 0)
            pe.wait_ge(folded, 4 * (1 + K))
            dense("res1", "res1r", [(w21, h0T), (w11, aggT)], colA, [h0_before, agg_block("agg1")])
            gather("agg2", T)
            dense("res2", "res2r", [(w22, h0T), (w12, aggT)], colA, [h0_before, agg_block("agg2")])
            for i, (stage, t) in enumerate(order[number["x2T", 0]:number["z", G * B - 1] + 1]):
                if stage == "x2T":
                    pe.wait_ge(ln_rows, T + t + 1)
                    tile_to_columns(stage, t)
                    continue
                if t == 0:
                    pe.wait_ge(wx_in, 16 * 4)
                n, g = t // G, t % G
                a, w = NBLK[n]
                if g == 0:
                    for m in range((a + w - 1) // R + 1):
                        wait_emptied(pe, "x2T", m)
                wait_bank(pe, "z", t)
                for k in range(K):
                    mm = nc.tensor.matmul(bank("z", t)[:, 0:w], wx[:, k, g // K, (g % K) * P:(g % K + 1) * P],
                                          xT[:, k, a:a + w], start=(k == 0), stop=(k == K - 1))
                fill(mm, "z", t)

            def unit(s, sw, i, _):
                if not sw.parts:
                    return
                a, w = WINS[i // K]
                j = i % K
                if j == 0:
                    pe.wait_ge(oper_ready, s * U + (i + K - U))
                pe.wait_ge(z_added, s * U + (i + 1 - U))
                for q in range(4):
                    for n, part in enumerate(sw.parts):
                        for k in range(K):
                            mm = nc.tensor.matmul(ps[:, 4 * (j % 2) + q, 0:w],
                                                  w_part[part][:, k, q, j * P:(j + 1) * P],
                                                  oper[sw.source][:, k, a:a + w], start=(n + k == 0),
                                                  stop=(n == len(sw.parts) - 1 and k == K - 1))
                mm.then_inc(unit_summed, 1)

            pe.wait_ge(low_ready, 4 * K)
            pe.wait_ge(started, 3)
            wait_first(pe, "z", G * B)
            all_sweeps(pe, unit, (0,), {10: lambda: pe.wait_ge(started, 4)})
            pe.wait_ge(z_added, 11 * U + 2)
            for t in range(T):
                pe.wait_ge(state_out, 5 * U + K * (1 + sum((t + 1) * R > a for a, _ in WINS[1:])))
                tile_to_rows("out", t, hT)
            pe.wait_ge(worst_ready, 1)
            nc.tensor.transpose(ps[0:1, 0, 0:P], worst[:, 0:1], ident[:, :]).then_inc(worst_turned, 1)
            pe.wait_ge(flag_ready, 1)
            with pe.If(pe.value_load(flag[0:1, 0:1], min_val=0, max_val=1) != 0):
                pe.wait_ge(wh_in, 16 * 4)
                with pe.Fori(0, N) as t:
                    pe.wait_ge(h_ready, t + 2)
                    for g in range(G):
                        for k in range(K):
                            mm = nc.tensor.matmul(ps[:, 0, g:g + 1], wh[:, k, g // K, (g % K) * P:(g % K + 1) * P],
                                                  h_now[:, k:k + 1], start=(k == 0), stop=(k == K - 1))
                    mm.then_inc(gates_ready, 1)
                pe.wait_ge(hT_ready, N)
                for t in range(T):
                    tile_to_rows("again", t, hT)

        @block.scalar
        def _(act):
            def roots(n, tiles):
                act.wait_ge(var_ready, n)
                r = rstd[0:R, tiles[0]:tiles[-1] + 1]
                nc.scalar.activation(r, r, ACT.Sqrt).then_inc(std_ready, 1)

            def column_out(stage, i, to, func, b):
                n, f = i // K, i % K
                a, w = NBLK[n]
                wait_filled(act, stage, i)
                empty(nc.scalar.activation(to[:, f, a:a + w], bank(stage, i)[:, 0:w], func,
                                           bias=bias[:, b + f:b + f + 1]), stage, i)

            def first_part(stage, t):
                if stage == "h0r":
                    wait_emptied(act, "norm", 0)
                wait_filled(act, stage, t)
                nc.scalar.activation(row_part[0][:, t, :], bank(stage, t)[0:R, :], ACT.Copy,
                                     scale=norm_c[0:R, t:t + 1]).then_inc(part1_ready, 1)

            def second_part(stage, t):
                wait_emptied(act, stage, t)
                nc.scalar.copy(row_part[1][:, t, :], left[t % 2]).then_inc(part2_ready, 1)

            def dense_out(stage, rows_, to, func, b):
                for st, i in turned(stage, rows_):
                    if st == stage:
                        column_out(stage, i, to, func, b)
                        continue
                    first_part(rows_, i)
                    if i > 0:
                        second_part(rows_, i - 1)
                second_part(rows_, T - 1)

            act.wait_ge(x_in, 16)
            for t in range(T):
                nc.scalar.activation(rows[:, t, :], xr[:, t, :], ACT.Identity, accum_out=sums[0:R, 0, t:t + 1])\
                    .then_inc(sums_ready, 1)
            act.wait_ge(means_ready, 1)
            act.wait_ge(sums_ready, T)
            for t in range(T):
                nc.scalar.activation(rows[:, t, :], xr[:, t, :], ACT.Square, bias=minus_mean[0:R, t:t + 1],
                                     accum_out=sums[0:R, 1, t:t + 1]).then_inc(squares_ready, 1)
            roots(1, range(T))
            with act.Fori(0, T // 2) as np_:
                for half in range(2):
                    n = np_ * 2 + half
                    act.wait_ge(counted, n + 1)
                    act.wait_ge(counts_split, n + 1)
                    for b in range(CB):
                        k = min(PER, T - b * PER)
                        nc.scalar.copy(block_counts[half][:, b * PER * R:(b * PER + k) * R],
                                       ps[0:R, CB * half + b, 0:k * R])
                        nc.scalar.copy(adj[0][:, b * PER:b * PER + k, bass.ds(n * R, R)],
                                       ps[0:R, CB * half + b, 0:k * R].rearrange("p (m d) -> p m d", m=k))
                    nc.scalar.copy(norm_b[:, bass.ds(n * R, R)],
                                   ps[:, CB * half + CB - 1, DEG_AT:DEG_AT + R]).then_inc(block_out, 1)
            act.wait_ge(scale_ready, 2)
            for t in range(T):
                nc.scalar.activation(rows[:, t, :], xr[:, t, :], ACT.Identity, bias=minus_mean[0:R, t:t + 1],
                                     scale=rstd[0:R, t:t + 1]).then_inc(ln_rows, 1)
            act.wait_ge(degrees_ready, 1)
            nc.scalar.activation(norm_b, norm_b, ACT.Sqrt).then_inc(root_ready, 1)
            wait_emptied(act, "bias", 0)
            dense_out("h0", "h0r", h0T, ACT.Identity, 0)
            dense_out("res1", "res1r", colA, ACT.Relu, K)
            for i in range(K * (B - 1)):
                column_out("res2", i, colA, ACT.Relu, 2 * K)
            roots(2, GROUPS[0])
            for i in range(K * (B - 1), K * B):
                column_out("res2", i, colA, ACT.Relu, 2 * K)
            roots(3, GROUPS[1])
            def second_split(m):
                act.wait_ge(rest_ready, m + 1)
                nc.scalar.copy(w_part[1][:, m // 4, m % 4, :], split[m % SLOTS]).then_inc(mid_ready, 1)

            def x_out(t):
                wait_filled(act, "x2T", t)
                empty(nc.scalar.copy(xT[:, :, t * R:(t + 1) * R],
                                     bank("x2T", t)[:, 0:K * R].rearrange("p (k r) -> p k r", k=K)), "x2T", t)

            def z_out(i):
                n, g = i // G, i % G
                a, w = NBLK[n]
                wait_filled(act, "z", i)
                empty(nc.scalar.activation(zT[:, g, a:a + w], bank("z", i)[:, 0:w], ACT.Identity,
                                           bias=bias[:, 3 * K + g:3 * K + g + 1]), "z", i)

            for t in GROUPS[0]:
                x_out(t)
            roots(4, GROUPS[2])
            for t in GROUPS[1]:
                x_out(t)
            m = 0
            for i in range(0, G * B, 2):
                if i == X_LATE:
                    for t in GROUPS[2]:
                        x_out(t)
                z_out(i)
                if m < 4 * K:
                    act.wait_ge(piece_in[m % SLOTS], 16 * (m // SLOTS + 1))
                    nc.scalar.copy(w_part[0][:, m // 4, m % 4, :], split[m % SLOTS]).then_inc(high_ready, 1)
                if 1 <= m <= 4 * K:
                    second_split(m - 1)
                m += 1

            def unit(s, sw, i, k):
                a, w = WINS[i // K]
                g = gate[i % LIVE][:, :, 0:w]
                if k == 0:
                    if sw.parts:
                        act.wait_ge(z_added, s * U + (i + 3 - U))
                    elif i >= LIVE:
                        act.wait_ge(oper_ready, i - LIVE + 1)
                    if sw.keep:
                        act.wait_ge(oper_ready, s * U + (i - LIVE + 1))
                    z = g if sw.parts and not sw.keep else z4[:, :, i % K, a:a + w]
                    nc.scalar.activation(g[:, 0:3, :], z[:, 0:3, :], ACT.Sigmoid).then_inc(unit_gated, 1)
                    nc.scalar.activation(g[:, 3, :], z[:, 3, :], ACT.Tanh).then_inc(unit_gated, 1)
                elif k == 1:
                    act.wait_ge(cells_ready, s * U + (i + 1))
                    nc.scalar.activation(g[:, 3, :], cells[:, i % K, 0:w], ACT.Tanh).then_inc(tanh_ready, 1)
                elif k == 3 and sw.to is None:
                    act.wait_ge(rest_taken, i + 1)
                    for n, r in enumerate((without_a[i % LIVE][:, 0:w], rest[i % LIVE][:, 0:w])):
                        ins = nc.scalar.activation(r, r, ACT.Square, accum_out=change[:, n, i:i + 1])
                    ins.then_inc(oper_ready, 1)

            act.wait_ge(started, 3)
            wait_first(act, "z", G * B)
            all_sweeps(act, unit, range(4))
            act.wait_ge(flag_ready, 1)
            with act.If(act.value_load(flag[0:1, 0:1], min_val=0, max_val=1) != 0):
                with act.Fori(0, N) as t:
                    act.wait_ge(z_ready, t + 1)
                    nc.scalar.activation(gates[:, 0:3 * K], z_now[:, 0:3 * K], ACT.Sigmoid).then_inc(act_ready, 1)
                    nc.scalar.activation(gates[:, 3 * K:G], z_now[:, 3 * K:G], ACT.Tanh).then_inc(act_ready, 1)
                    act.wait_ge(c_ready, t + 1)
                    nc.scalar.activation(tc[:, :], cell[:, :], ACT.Tanh).then_inc(tc_ready, 1)

        @block.vector
        def _(dve):
            link_n = [0]

            def link(ins):
                link_n[0] += 1
                ins.then_inc(chained, 1)
                dve.wait_ge(chained, link_n[0])

            def normalize(n, tiles):
                for t in tiles:
                    wait_filled(dve, "res2r", t)
                    empty(nc.vector.tensor_tensor(xr[:, t, :], xr[:, t, :], bank("res2r", t)[0:R, :], ALU.add),
                          "res2r", t)
                for t in tiles:
                    wait_emptied(dve, "res2r", t)
                    nc.vector.bn_stats(stats[0:R, t, :], xr[:, t, :]).then_inc(stat_ready, 1)
                dve.wait_ge(stat_ready, tiles[-1] + 1)
                for t in tiles:
                    ins = nc.vector.bn_aggr(mv[0:R, t, :], stats[0:R, t, :])
                link(ins)
                r = rstd[0:R, tiles[0]:tiles[-1] + 1]
                nc.vector.tensor_scalar(r, mv[0:R, tiles[0]:tiles[-1] + 1, 1], EPS, None, ALU.add)\
                    .then_inc(var_ready, 1)
                dve.wait_ge(std_ready, n)
                link(nc.vector.reciprocal(r, r))
                for t in tiles:
                    nc.vector.tensor_scalar(rows[:, t, :], xr[:, t, :], mv[0:R, t, 0:1], rstd[0:R, t:t + 1],
                                            ALU.subtract, ALU.mult).then_inc(ln_rows, 1)

            def left_out(stage, n_before):
                for t in range(T):
                    n = n_before + t
                    dve.wait_ge(part1_ready, n + 1)
                    if n >= 2:
                        dve.wait_ge(part3_ready, n - 1)
                    empty(nc.vector.scalar_tensor_tensor(out=left[t % 2], in0=bank(stage, t)[0:R, :],
                                                         scalar=norm_c[0:R, t:t + 1], in1=row_part[0][:, t, :],
                                                         op0=ALU.mult, op1=ALU.subtract), stage, t)

            def sums_out(stage):
                for f in range(K):
                    for n, (a, w) in enumerate(NBLK):
                        wait_filled(dve, stage, f * B + n)
                        empty(nc.vector.scalar_tensor_tensor(
                            out=aggT[:, f, a:a + w], in0=bank(stage, f * B + n)[:, 0:w], scalar=1.0 - ALPHA,
                            in1=norm_b[:, a:a + w], op0=ALU.mult, op1=ALU.mult), stage, f * B + n)

            dve.wait_ge(edges_in, 32)
            for s in range(2):
                nc.vector.tensor_copy(edge_f[s], edge_i[s]).then_inc(edges_f, 1)
            nc.vector.memset(zeros[:, :], 0.0).then_inc(zeros_ready, 1)
            for n in range(2):
                nc.vector.memset(change[:, n, :], 0.0).then_inc(block_out, 1)
            for n in range(4):
                nc.vector.memset(hot_src[n], 0.0).then_inc(hot_used, 1)
            dve.wait_ge(edges_f, 2)
            nc.vector.tensor_reduce(reach[:, 0:1], edge_f[1], AX.X, ALU.min)
            link(nc.vector.tensor_reduce(reach[:, 1:2], edge_f[1], AX.X, ALU.max))
            dve.wait_ge(consts, 7)
            nc.vector.tensor_scalar(meets[:, 0, :], block_at, reach[:, 1:2], None, ALU.is_le)
            link(nc.vector.tensor_scalar(meets[:, 1, :], block_at, float(R - 1), reach[:, 0:1], ALU.add, ALU.is_ge))
            link(nc.vector.tensor_tensor(meets[:, 0, :], meets[:, 0, :], meets[:, 1, :], ALU.mult))
            nc.vector.tensor_scalar(keys[:, 0, :], meets[:, 0, :], pair_up, None, ALU.mult).then_inc(keys_ready, 1)
            nc.vector.tensor_scalar(keys[:, 1, :], meets[:, 0, :], pair_down, None, ALU.mult).then_inc(keys_ready, 1)
            dve.wait_ge(edges_turned, 1)
            nc.vector.tensor_copy(edge_c.rearrange("p s h e -> p (s h e)"),
                                  ps[0:R, BANKS - 1, 0:4 * EP]).then_inc(edges_ready, 1)
            dve.wait_ge(ends_ready, 1)
            link(nc.vector.tensor_scalar(ends[0:1, 0, :], ends[0:1, 0, :], 1.0, None, ALU.max))
            link(nc.vector.tensor_scalar(ends[0:1, 1, :], ends[0:1, 1, :], -1.0, float(EP), ALU.mult, ALU.add))
            link(nc.vector.scalar_tensor_tensor(out=span[:, 0, :], in0=ends[0:1, 0, :], scalar=-1.0,
                                                in1=ends[0:1, 1, :], op0=ALU.add, op1=ALU.min))
            link(nc.vector.tensor_tensor(span_up, ends[0:1, 0, :], span[:, 0, :], ALU.subtract))
            link(nc.vector.tensor_scalar(halves, span_up, 1.0, None, ALU.add))
            link(nc.vector.tensor_scalar(halves, halves, 1, None, ALU.arith_shift_right))
            link(nc.vector.tensor_copy(span[:, 1, :], halves))
            link(nc.vector.tensor_scalar(span_up, span[:, 1, :], -2.0, float(EP), ALU.mult, ALU.add))
            link(nc.vector.tensor_tensor(span[:, 0, :], span[:, 0, :], span_up, ALU.min))
            link(nc.vector.tensor_tensor_scan(meets[0:1, 0, :], ones_f[:, :], span[:, 1, :], 0.0,
                                              ALU.mult, ALU.add))
            link(nc.vector.tensor_tensor(span[:, 2, :], meets[0:1, 0, :], span[:, 1, :], ALU.subtract))
            nc.vector.tensor_copy(spans[:, :, :], span[:, :, :]).then_inc(spans_ready, 1)
            dve.wait_ge(edges_ready, 1)
            dve.wait_ge(spans_ready, 1)
            with dve.Fori(0, T) as n:
                first_pair = dve.value_load(spans[0:1, 0, bass.ds(n, 1)], min_val=0, max_val=EP - 2)
                count = dve.value_load(spans[0:1, 1, bass.ds(n, 1)], min_val=1, max_val=EP // 2)
                base = dve.value_load(spans[0:1, 2, bass.ds(n, 1)], min_val=0, max_val=T * EP)
                with dve.Fori(0, count) as i:
                    for k in range(4):
                        dve.wait_ge(hot_used, (base + i) * 4 + (k + 1))
                        e = nc.s_assert_within(first_pair + i * 2 + k // 2, 0, EP - 1,
                                               skip_runtime_bounds_check_because="a span ends at the last pair")
                        nc.vector.tensor_scalar(hot_dst[k], iota[:, bass.ds(n * R, R)],
                                                edge_c[:, 1, k % 2, bass.ds(e, 1)], None, ALU.is_equal)
                        nc.vector.tensor_scalar(hot_src[k], iota, edge_c[:, 0, k % 2, bass.ds(e, 1)], None,
                                                ALU.is_equal).then_inc(hot_ready, 1)
            dve.wait_ge(std_ready, 1)
            nc.vector.reciprocal(rstd[0:R, :], rstd[0:R, :]).then_inc(scale_ready, 1)
            dve.wait_ge(scale_ready, 1)
            nc.vector.tensor_tensor(minus_mean[0:R, :], minus_mean[0:R, :], rstd[0:R, :], ALU.mult)\
                .then_inc(scale_ready, 1)
            dve.wait_ge(block_out, T + 2)
            nc.vector.tensor_scalar(norm_b, norm_b, 1.0, None, ALU.max).then_inc(degrees_ready, 1)
            wait_filled(dve, "bias", 0)
            empty(nc.vector.tensor_copy(bias[:, :], bank("bias", 0)[:, 0:3 * K + G]), "bias", 0)
            for o in range(K):
                wait_filled(dve, "fct", o)
                empty(nc.vector.tensor_copy(fct[:, :, o * P:(o + 1) * P],
                                            bank("fct", o).rearrange("p (k d) -> p k d", k=K)), "fct", o)
            dve.wait_ge(counts_split, T + 2)
            for t in range(T):
                wait_filled(dve, "xT", t)
                empty(nc.vector.tensor_copy(colA[:, :, t * R:(t + 1) * R],
                                            bank("xT", t)[:, 0:K * R].rearrange("p (k r) -> p k r", k=K)), "xT", t)
            dve.wait_ge(root_ready, 1)
            nc.vector.reciprocal(norm_b, norm_b).then_inc(norm_ready, 1)
            wait_filled(dve, "norm", 0)
            ins = nc.vector.tensor_copy(norm_c[0:R, :], bank("norm", 0)[0:R, 0:T])
            empty(ins, "norm", 0)
            wait_emptied(dve, "norm", 0)
            nc.vector.tensor_reduce(most_of[0:R, :], adj[0].rearrange("p t n -> p (t n)"), AX.X, ALU.max)\
                .then_inc(most_ready, 1)
            dve.wait_ge(norm_ready, 1)
            left_out("h0r", 0)
            wait_filled(dve, "most", 0)
            empty(nc.vector.tensor_reduce(most[:, :], bank("most", 0)[0:1, 0:R], AX.X, ALU.max), "most", 0)
            wait_emptied(dve, "most", 0)
            nc.vector.tensor_scalar(many_flag[:, :], most[:, :], 255.0, None, ALU.is_gt).then_inc(many_ready, 1)
            dve.wait_ge(w_in, 16 * 5)
            n = 0
            for layer, pair in ((1, (w11, w21)), (2, (w12, w22))):
                beta = math.log(LAMBDA / layer + 1.0)
                for w, c in zip(pair, (1.0, ALPHA)):
                    nc.vector.tensor_scalar(w, w, c * beta, None, ALU.mult).then_inc(folded, 1)
                    n += 1
                    dve.wait_ge(folded, n)
                    for k in range(K):
                        d = w[:, k, k * P:(k + 1) * P]
                        nc.vector.scalar_tensor_tensor(out=d, in0=ident[:, :], scalar=c * (1.0 - beta), in1=d,
                                                       op0=ALU.mult, op1=ALU.add).then_inc(folded, 1)
                        n += 1
            sums_out("agg1")
            left_out("res1r", T)
            sums_out("agg2")
            for n, tiles in enumerate(GROUPS):
                normalize(2 + n, tiles)

            def z_out(i):
                n, g = i // G, i % G
                a, w = NBLK[n]
                wait_filled(dve, "z", i)
                empty(nc.vector.tensor_scalar(zT[:, g, a:a + w], bank("z", i)[:, 0:w],
                                              bias[:, 3 * K + g:3 * K + g + 1], None, ALU.add), "z", i)

            def third_split(m):
                dve.wait_ge(mid_ready, m + 1)
                nc.vector.tensor_tensor(w_part[2][:, m // 4, m % 4, :], split[m % SLOTS],
                                        w_part[1][:, m // 4, m % 4, :], ALU.subtract).then_inc(low_ready, 1)

            for m, i in enumerate(range(1, G * B, 2)):
                z_out(i)
                if m < 4 * K:
                    dve.wait_ge(high_ready, m + 1)
                    nc.vector.tensor_tensor(split[m % SLOTS], split[m % SLOTS],
                                            w_part[0][:, m // 4, m % 4, :], ALU.subtract).then_inc(rest_ready, 1)
                if 1 <= m <= 4 * K:
                    third_split(m - 1)
            wait_first(dve, "z", G * B)
            dve.wait_ge(low_ready, 4 * K)
            for o in range(3):
                nc.vector.memset(oper[o][:, :, 0:1], 0.0).then_inc(started, 1)
            for n in range(2):
                nc.vector.memset(change[:, n, :], 0.0).then_inc(z_added, 1)

            diffs = [0]

            def unit(s, sw, i, k):
                a, w = WINS[i // K]
                j = i % K
                g = gate[i % LIVE][:, :, 0:w]
                if k == 0 and sw.parts:
                    z = z4[:, :, j, a:a + w]
                    half = 4 * (j % 2)
                    if sw.third_free and (i >= LIVE or len(sw.taken) > 1):
                        dve.wait_ge(state_out, (s - 6) * U + (i - LIVE + 1))
                    else:
                        dve.wait_ge(oper_ready, s * U + (i - LIVE + 1))
                    dve.wait_ge(unit_summed, s * U + (i + 1 - U))
                    nc.vector.tensor_tensor(z if sw.keep else g, z, ps[:, half:half + 4, 0:w], ALU.add)\
                        .then_inc(z_added, 1)
                if k == 1:
                    last = WINS[i // K - 1][1]
                    dve.wait_ge(ig_ready, s * U + (i + 1))
                    if i >= K:
                        dve.wait_ge(tanh_ready, s * U + (i - K + 1))
                        dve.wait_ge(cells_ready, s * U + (i - K + 1))
                    nc.vector.tensor_tensor_scan(cells[:, j, 0:w], g[:, 0, :], g[:, 1, :],
                                                 0.0 if i < K else cells[:, j, last - 1:last],
                                                 ALU.mult, ALU.add).then_inc(cells_ready, 1)
                if sw.taken and k == (2 if len(sw.taken) == 1 else 3):
                    if sw.third_free and len(sw.taken) == 1:
                        dve.wait_ge(state_out, (s - 6) * U + (i + 1))
                    else:
                        dve.wait_ge(hidden_ready, (0 if len(sw.taken) == 1 else s - 8) * U + (i + 1))
                    taken = sw.taken[1:] or sw.taken
                    h = state[i % LIVE][:, 0:w] if sw.third_free else g[:, 2, :]
                    for n, o in enumerate(taken):
                        final = n == len(taken) - 1
                        if sw.to is None:
                            h = rest[i % LIVE][:, 0:w] if n else without_a[i % LIVE][:, 0:w]
                            to, done = rest[i % LIVE][:, 0:w], rest_taken if final else diff_step
                        else:
                            to, done = oper[sw.to][:, j, 1 + a:1 + a + w], oper_ready
                        if n:
                            dve.wait_ge(diff_step, diffs[0])
                        nc.vector.tensor_tensor(to, h, oper[o][:, j, 1 + a:1 + a + w], ALU.subtract)\
                            .then_inc(done, 1)
                        diffs[0] += int(not final)

            def zero_e():
                nc.vector.memset(oper[E_][:, :, 0:1], 0.0).then_inc(started, 1)

            all_sweeps(dve, unit, range(4), {5: lambda: dve.wait_ge(zx_saved, 16), 8: zero_e})
            for t in range(T):
                wait_filled(dve, "out", t)
                empty(nc.vector.tensor_tensor(out_rows[:, t, :], xr[:, t, :], bank("out", t)[0:R, :], ALU.add),
                      "out", t)
            dve.wait_ge(oper_ready, 12 * U)
            for n in range(2):
                nc.vector.tensor_reduce(worst[:, n:n + 1], change[:, n, :], AX.X, ALU.max).then_inc(diff_step, 1)
            diffs[0] += 2
            dve.wait_ge(diff_step, diffs[0])
            nc.vector.tensor_scalar(worst[:, :], worst[:, :], 1.0 / CHANGE_LIMIT ** 2, None, ALU.mult).then_inc(diff_step, 1)
            diffs[0] += 1
            dve.wait_ge(diff_step, diffs[0])
            nc.vector.scalar_tensor_tensor(out=worst[:, 0:1], in0=worst[:, 0:1], scalar=(CHANGE_LIMIT / REST_LIMIT) ** 2,
                                           in1=worst[:, 1:2], op0=ALU.mult, op1=ALU.max).then_inc(worst_ready, 1)
            dve.wait_ge(worst_turned, 1)
            nc.vector.tensor_reduce(far[:, :], ps[0:1, 0, 0:P], AX.X, ALU.max).then_inc(diff_step, 1)
            diffs[0] += 1
            dve.wait_ge(diff_step, diffs[0])
            nc.vector.tensor_scalar(flag[:, :], far[:, :], 1.0, None, ALU.is_gt).then_inc(flag_ready, 1)
            dve.wait_ge(flag_ready, 1)
            with dve.If(dve.value_load(flag[0:1, 0:1], min_val=0, max_val=1) != 0):
                dve.wait_ge(zx_back, 16)
                nc.vector.memset(cell[:, :], 0.0).then_inc(h_ready, 1)
                nc.vector.memset(h_now[:, :], 0.0).then_inc(h_ready, 1)
                dve.wait_ge(h_ready, 2)
                with dve.Fori(0, N) as t:
                    dve.wait_ge(gates_ready, t + 1)
                    z_t = zT[:, :, bass.ds(t, 1)].rearrange("p g o -> p (g o)")
                    nc.vector.tensor_tensor(z_now[:, :], z_t, ps[:, 0, 0:G], ALU.add).then_inc(z_ready, 1)
                    dve.wait_ge(act_ready, t * 2 + 2)
                    nc.vector.tensor_tensor(ig[:, :], gates[:, K:2 * K], gates[:, 3 * K:G], ALU.mult).then_inc(cell_step, 1)
                    nc.vector.tensor_tensor(fc[:, :], gates[:, 0:K], cell[:, :], ALU.mult).then_inc(cell_step, 1)
                    dve.wait_ge(cell_step, t * 2 + 2)
                    nc.vector.tensor_tensor(cell[:, :], ig[:, :], fc[:, :], ALU.add).then_inc(c_ready, 1)
                    dve.wait_ge(tc_ready, t + 1)
                    dve.wait_ge(c_ready, t + 1)
                    nc.vector.tensor_tensor(h_now[:, :], gates[:, 2 * K:3 * K], tc[:, :], ALU.mult).then_inc(h_ready, 1)
                    h_t = hT[:, :, bass.ds(t, 1)].rearrange("p k o -> p (k o)")
                    nc.vector.tensor_tensor(h_t, gates[:, 2 * K:3 * K], tc[:, :], ALU.mult).then_inc(hT_ready, 1)
                for t in range(T):
                    wait_filled(dve, "again", t)
                    empty(nc.vector.tensor_tensor(xr[:, t, :], xr[:, t, :], bank("again", t)[0:R, :], ALU.add),
                          "again", t)


_INS = ["x", "src", "dst", "L0_gnn_fc_w", "L0_gnn_fc_b", "L0_gnn_w1_1", "L0_gnn_w2_1", "L0_gnn_b_1",
        "L0_gnn_w1_2", "L0_gnn_w2_2", "L0_gnn_b_2", "L0_ffn_W_f", "L0_ffn_b_f", "L0_ffn_W_i", "L0_ffn_b_i",
        "L0_ffn_W_c", "L0_ffn_b_c", "L0_ffn_W_o", "L0_ffn_b_o"]


def kernel(**inputs):
    import numpy as np
    import concourse.bacc as bacc
    from concourse import mybir as mb
    from concourse.bass_utils import run_bass_kernel_spmd

    nc = bacc.Bacc("TRN2", target_bir_lowering=False, num_devices=1)
    arrays, args = {}, []
    for name in _INS:
        a = np.ascontiguousarray(inputs[name])
        arrays[f"in_{name}"] = a
        args.append(nc.dram_tensor(f"in_{name}", a.shape, mb.dt.from_np(a.dtype), kind="ExternalInput").ap())
    out = nc.dram_tensor("out_0", inputs["x"].shape, mb.dt.float32, kind="ExternalOutput").ap()
    gnn_lstm_kernel(nc, *args, out)
    return run_bass_kernel_spmd(nc, [arrays], core_ids=[0]).results[0]["out_0"]
```
